# Optimizing a Trainium2 kernel written in Bass

```python
import numpy as np
import jax
import jax.numpy as jnp

def _softmax(x, axis=-1):
    return jax.nn.softmax(x, axis=axis)

def _gelu(x):
    return jax.nn.gelu(x, approximate=True)

def _silu(x):
    return jax.nn.silu(x)

def _sigmoid(x):
    return jax.nn.sigmoid(x)

def _layernorm(x, axis=-1, eps=1e-05):
    m = jnp.mean(x, axis=axis, keepdims=True)
    v = jnp.var(x, axis=axis, keepdims=True)
    return (x - m) / jnp.sqrt(v + eps)

def _scatter_add(tgt, idx, src, axis=0):
    return tgt.at[idx].add(src)

def _segment_sum(src, seg, n):
    return jax.ops.segment_sum(src, seg, n)
kernel_name = 'mk_perceiver_d1_seqx_r2_97bf9a'

def setup_inputs(seed: int=0):
    np.random.seed(seed)
    _w = jnp.asarray

    def _rec_inputs():
        import jax
        import jax.numpy as jnp
        _rk = jax.random.key(seed)
        x = -0.0002928 + 1 * jax.random.normal(jax.random.fold_in(_rk, 1), (4, 128, 512), jnp.float32)
        _lenS = 128 - jax.random.randint(jax.random.fold_in(_rk, 7), (4,), 0, max(1, 128 // 4) + 1, jnp.int32)
        _lenS2 = 2048 - jax.random.randint(jax.random.fold_in(_rk, 8), (4,), 0, max(1, 2048 // 4) + 1, jnp.int32)
        _ctx_1024P = jax.random.normal(jax.random.fold_in(_rk, 11), (4, 16, 512), jnp.float32)
        _ctx_1024c = jax.random.dirichlet(jax.random.fold_in(_rk, 511), 0.3 * jnp.ones((16,), jnp.float32), (4, 2048))
        _ctx_1024t = jnp.einsum('bsk,bkd->bsd', _ctx_1024c, _ctx_1024P)
        _ctx_1024t = _ctx_1024t * jax.lax.rsqrt(jnp.mean(jnp.square(_ctx_1024t)) + 1e-12) * 0.953939
        ctx_1024 = -1.39393e-06 + 0.999914 * (_ctx_1024t + 0.3 * jax.random.normal(jax.random.fold_in(_rk, 611), (4, 2048, 512), jnp.float32))
        fside_BxS2_0 = 0.0132156 + 1.00766 * jax.random.normal(jax.random.fold_in(_rk, 12), (4, 2048), jnp.float32)
        _validS = jnp.arange(128)[None, :] < _lenS[:, None]
        _validS2 = jnp.arange(2048)[None, :] < _lenS2[:, None]
        _causal = jnp.tril(jnp.ones((128, 128), dtype=bool))
        mask_BxS2_bk0 = jnp.logical_not(jnp.broadcast_to(_validS2[:, :], (4, 2048)))
        return (x, ctx_1024, fside_BxS2_0, mask_BxS2_bk0)
    x, ctx_1024, fside_BxS2_0, mask_BxS2_bk0 = _rec_inputs()

    def _L0_xattn_setup():
        import jax, jax.numpy as jnp
        import numpy as np
        EMBED_DIM = 512
        NUM_HEADS = 16
        HEAD_DIM = EMBED_DIM // NUM_HEADS
        B, SQ, SK = (2, 1024, 1024)
        key = jax.random.key(seed)
        ks = jax.random.split(key, 10)
        s = 1.0 / np.sqrt(EMBED_DIM)
        return {'tgt': jax.random.normal(ks[0], (B, SQ, EMBED_DIM), jnp.float32), 'mem': jax.random.normal(ks[1], (B, SK, EMBED_DIM), jnp.float32), 'attn_bias': jax.random.normal(ks[2], (B, SK), jnp.float32), 'memory_key_padding_mask': jax.random.randint(ks[3], (B, SK), 0, 2).astype(bool), 'Wq_w': jax.random.normal(ks[4], (EMBED_DIM, EMBED_DIM), jnp.float32) * s, 'Wq_b': jnp.zeros((EMBED_DIM,), jnp.float32), 'Wkv_w': jax.random.normal(ks[5], (2 * EMBED_DIM, EMBED_DIM), jnp.float32) * s, 'Wkv_b': jnp.zeros((2 * EMBED_DIM,), jnp.float32), 'out_w': jax.random.normal(ks[6], (EMBED_DIM, EMBED_DIM), jnp.float32) * s, 'out_b': jnp.zeros((EMBED_DIM,), jnp.float32)}
    _L0_xattn_all = _L0_xattn_setup()
    _L0_xattn_in = {k: v for k, v in _L0_xattn_all.items() if k in ('Wq_w', 'Wq_b', 'Wkv_w', 'Wkv_b', 'out_w', 'out_b')}
    del _L0_xattn_all

    def _L0_attn_setup():
        import jax, jax.numpy as jnp
        import numpy as np
        B, T, D, H = (2, 1024, 512, 16)
        DH = D // H
        EPS = 1e-07
        HI = 1.0 - 1e-07

        def _clamp(x):
            return jnp.clip(x, EPS, HI)

        def _clamp_nan(x):
            return jnp.nan_to_num(jnp.clip(x, EPS, HI), nan=0.0)
        key = jax.random.key(seed)
        ks = jax.random.split(key, 9)
        s = 0.02
        return {'hidden_states': jax.random.normal(ks[0], (B, T, D), jnp.float32), 'Wq': jax.random.normal(ks[1], (D, D), jnp.float32) * s, 'bq': jax.random.normal(ks[2], (D,), jnp.float32) * s, 'Wk': jax.random.normal(ks[3], (D, D), jnp.float32) * s, 'bk': jax.random.normal(ks[4], (D,), jnp.float32) * s, 'Wv': jax.random.normal(ks[5], (D, D), jnp.float32) * s, 'bv': jax.random.normal(ks[6], (D,), jnp.float32) * s, 'Wo': jax.random.normal(ks[7], (D, D), jnp.float32) * s, 'bo': jax.random.normal(ks[8], (D,), jnp.float32) * s}
    _L0_attn_all = _L0_attn_setup()
    _L0_attn_in = {k: v for k, v in _L0_attn_all.items() if k in ('Wq', 'bq', 'Wk', 'bk', 'Wv', 'bv', 'Wo', 'bo')}
    del _L0_attn_all

    def _L0_ffn_setup():
        import jax, jax.numpy as jnp
        import numpy as np
        N, T, D = (4, 2048, 512)
        NUM_EXPERTS = 8
        EXPERT_CAP = 2.0
        MLP_RATIO = 4
        HIDDEN = MLP_RATIO * D
        key = jax.random.key(seed)
        k1, k2, k3, k4 = jax.random.split(key, 4)
        x = jax.random.normal(k1, (N, T, D), dtype=jnp.float32)
        gate_w = jax.random.truncated_normal(k2, -2.0, 2.0, (D, NUM_EXPERTS), dtype=jnp.float32) * 0.02
        w1 = jax.random.normal(k3, (NUM_EXPERTS, D, HIDDEN), dtype=jnp.float32) * 0.02
        w2 = jax.random.normal(k4, (NUM_EXPERTS, HIDDEN, D), dtype=jnp.float32) * 0.02
        return {'x': x, 'gate_w': gate_w, 'w1': w1, 'w2': w2}
    _L0_ffn_all = _L0_ffn_setup()
    _L0_ffn_in = {k: v for k, v in _L0_ffn_all.items() if k in ('gate_w', 'w1', 'w2')}
    del _L0_ffn_all
    return {'x': x, 'ctx_1024': ctx_1024, 'fside_BxS2_0': fside_BxS2_0, 'mask_BxS2_bk0': mask_BxS2_bk0, 'L0_xattn_Wq_w': _L0_xattn_in['Wq_w'], 'L0_xattn_Wq_b': _L0_xattn_in['Wq_b'], 'L0_xattn_Wkv_w': _L0_xattn_in['Wkv_w'], 'L0_xattn_Wkv_b': _L0_xattn_in['Wkv_b'], 'L0_xattn_out_w': _L0_xattn_in['out_w'], 'L0_xattn_out_b': _L0_xattn_in['out_b'], 'L0_attn_Wq': _L0_attn_in['Wq'], 'L0_attn_bq': _L0_attn_in['bq'], 'L0_attn_Wk': _L0_attn_in['Wk'], 'L0_attn_bk': _L0_attn_in['bk'], 'L0_attn_Wv': _L0_attn_in['Wv'], 'L0_attn_bv': _L0_attn_in['bv'], 'L0_attn_Wo': _L0_attn_in['Wo'], 'L0_attn_bo': _L0_attn_in['bo'], 'L0_ffn_gate_w': _L0_ffn_in['gate_w'], 'L0_ffn_w1': _L0_ffn_in['w1'], 'L0_ffn_w2': _L0_ffn_in['w2']}

def reference(x, ctx_1024, fside_BxS2_0, mask_BxS2_bk0, L0_xattn_Wq_w, L0_xattn_Wq_b, L0_xattn_Wkv_w, L0_xattn_Wkv_b, L0_xattn_out_w, L0_xattn_out_b, L0_attn_Wq, L0_attn_bq, L0_attn_Wk, L0_attn_bk, L0_attn_Wv, L0_attn_bv, L0_attn_Wo, L0_attn_bo, L0_ffn_gate_w, L0_ffn_w1, L0_ffn_w2):
    import jax
    import jax.numpy as jnp

    def _L0_xattn_ref(tgt, mem, attn_bias, memory_key_padding_mask, Wq_w, Wq_b, Wkv_w, Wkv_b, out_w, out_b):
        import jax, jax.numpy as jnp
        import numpy as np
        EMBED_DIM = 512
        NUM_HEADS = 16
        HEAD_DIM = EMBED_DIM // NUM_HEADS
        B, SQ, SK = (2, 1024, 1024)
        b, sq, _ = tgt.shape
        sk = mem.shape[1]
        q = (tgt @ Wq_w.T + Wq_b).reshape(b, sq, NUM_HEADS, HEAD_DIM)
        kv = (mem @ Wkv_w.T + Wkv_b).reshape(b, sk, 2, NUM_HEADS, HEAD_DIM)
        k, v = (kv[:, :, 0], kv[:, :, 1])
        scale = 1.0 / np.sqrt(HEAD_DIM)
        scores = jnp.einsum('bthd,bshd->bhts', q, k * scale)
        scores = scores + attn_bias[:, None, None, :]
        pad = jnp.where(memory_key_padding_mask, 0.0, -jnp.inf).astype(scores.dtype)
        scores = scores + pad[:, None, None, :]
        attn = jax.nn.softmax(scores, axis=-1)
        ctx = jnp.einsum('bhts,bshd->bthd', attn, v)
        out = ctx.reshape(b, sq, EMBED_DIM) @ out_w.T + out_b
        return out

    def _L0_attn_ref(hidden_states, Wq, bq, Wk, bk, Wv, bv, Wo, bo):
        import jax, jax.numpy as jnp
        import numpy as np
        B, T, D, H = (2, 1024, 512, 16)
        DH = D // H
        EPS = 1e-07
        HI = 1.0 - 1e-07

        def _clamp(x):
            return jnp.clip(x, EPS, HI)

        def _clamp_nan(x):
            return jnp.nan_to_num(jnp.clip(x, EPS, HI), nan=0.0)
        b, t, d = hidden_states.shape
        scaling = DH ** (-0.5)

        def heads(x):
            return x.reshape(b, t, H, DH).transpose(0, 2, 1, 3)
        q = _clamp_nan(heads((hidden_states @ Wq.T + bq) * scaling))
        k = _clamp_nan(heads(hidden_states @ Wk.T + bk))
        v = _clamp_nan(heads(hidden_states @ Wv.T + bv))
        attn_weights = _clamp(jnp.einsum('bhtd,bhsd->bhts', q, k))
        attn_probs = _clamp(jax.nn.softmax(attn_weights, axis=-1))
        attn_out = _clamp(jnp.einsum('bhts,bhsd->bhtd', attn_probs, v))
        attn_out = attn_out.transpose(0, 2, 1, 3).reshape(b, t, d)
        return _clamp_nan(attn_out @ Wo.T + bo)

    def _L0_ffn_ref(x, gate_w, w1, w2):
        import jax, jax.numpy as jnp
        import numpy as np
        N, T, D = (4, 2048, 512)
        NUM_EXPERTS = 8
        EXPERT_CAP = 2.0
        MLP_RATIO = 4
        HIDDEN = MLP_RATIO * D
        x = x.astype(jnp.float32)
        n, t, d = x.shape
        k = int(EXPERT_CAP * t / NUM_EXPERTS)
        scores = jnp.einsum('ntd,de->nte', x, gate_w)
        probs = jax.nn.softmax(scores, axis=-1)
        probs = jnp.transpose(probs, (0, 2, 1))
        g, m = jax.lax.top_k(probs, k)
        xin = jax.vmap(lambda xb, mb: xb[mb])(x, m)
        h = jax.nn.gelu(jnp.einsum('nekd,edf->nekf', xin, w1))
        h = jnp.einsum('nekf,efd->nekd', h, w2)
        weighted = g[..., None] * h
        flat_idx = (m + jnp.arange(n, dtype=m.dtype)[:, None, None] * t).reshape(-1)
        out = jnp.zeros((n * t, d), dtype=jnp.float32).at[flat_idx].add(weighted.reshape(-1, d))
        out = out.reshape(n, t, d)
        return out.astype(jnp.bfloat16)
    x = x + _L0_xattn_ref(_layernorm(x, axis=-1), ctx_1024, fside_BxS2_0, mask_BxS2_bk0, L0_xattn_Wq_w, L0_xattn_Wq_b, L0_xattn_Wkv_w, L0_xattn_Wkv_b, L0_xattn_out_w, L0_xattn_out_b)
    x = x + _L0_attn_ref(_layernorm(x, axis=-1), L0_attn_Wq, L0_attn_bq, L0_attn_Wk, L0_attn_bk, L0_attn_Wv, L0_attn_bv, L0_attn_Wo, L0_attn_bo)
    x = x + _L0_ffn_ref(_layernorm(x, axis=-1), L0_ffn_gate_w, L0_ffn_w1, L0_ffn_w2)
    return x

_drawn_inputs = setup_inputs


def setup_inputs(seed=0):
    import zlib

    import numpy as np

    out = dict(_drawn_inputs(seed))
    spreads = {'L0_xattn_Wq_b': (0.0, 0.392), 'L0_xattn_Wkv_b': (0.0, 0.1), 'L0_xattn_out_b': (0.0, 0.1)}
    factors = {'L0_attn_Wq': 8.0,
     'L0_attn_bq': 8.0,
     'L0_attn_Wk': 8.0,
     'L0_attn_bk': 8.0,
     'L0_attn_bv': 8.0,
     'L0_attn_bo': 5.032}
    for name, (base, spread) in spreads.items():
        noise = np.random.default_rng([zlib.crc32(name.encode()), seed]).standard_normal(out[name].shape)
        drawn = base * np.exp(spread * noise) if base else spread * noise
        out[name] = jnp.asarray(drawn.astype(out[name].dtype))
    for name, factor in factors.items():
        out[name] = (out[name] * factor).astype(out[name].dtype)
    return out
```

```python
from contextlib import ExitStack

import concourse.bass as bass
from concourse import mybir

ALU = mybir.AluOpType
ACT = mybir.ActivationFunctionType
AX = mybir.AxisListType
F32 = mybir.dt.float32
BF16 = mybir.dt.bfloat16
I32 = mybir.dt.int32
U8 = mybir.dt.uint8

P = 128
B, T, D = 4, 128, 512
SK = 2048
H, DH = 16, 32
KC = D // P
NCH = SK // P
NJ = B * NCH
STRIPS = P // DH
E, F = 8, 2048
CAP = 2 * T // E
FC = F // P
HV = DH + 1
MASKED = 1.0e30
EPS_LN = 1e-5
LO, HI = 1e-7, 1.0 - 1e-7
SCALE = DH ** -0.5


def decoder_layer(nc, x, ctx_t, key_bias, key_mask, wq, bq, wk, bk, wv, bv, wo, bo,
                  sq, sbq, sk, sbk, sv, sbv, so, sbo, gate, w1, w2, out):
    with ExitStack() as ctx:
        def sb(name, shape, dt=F32):
            return ctx.enter_context(nc.sbuf_tensor(name, shape, dt))

        def sem(name):
            return ctx.enter_context(nc.semaphore(name))

        att_w = sb("att_w", [P, 8, KC, D])
        wq_s, wk_s, wv_s, wo_s, sq_s, sk_s, sv_s, so_s = (att_w[:, i] for i in range(8))
        ffn_a = sb("ffn_a", [P, 2, KC * F])
        flat = att_w[:].rearrange("p a k n -> p (a k n)").rearrange("p (i n) -> p i n", i=2)
        w1_s = [ffn_a[:, 0, :].rearrange("p (k f) -> p k f", k=KC), flat[:, 0, :].rearrange("p (k f) -> p k f", k=KC)]
        w2_s = [ffn_a[:, 1, :].rearrange("p (c n) -> p c n", c=FC), flat[:, 1, :].rearrange("p (c n) -> p c n", c=FC)]

        x_s = sb("x_s", [P, B, D])
        norm = sb("norm", [P, B, D])
        tr = sb("tr", [P, KC, B * T])
        qk = sb("qk", [P, 2, B, KC, T])
        qt, kt2 = qk[:, 0], qk[:, 1]
        big_a = sb("big_a", [P, H, P])
        big_b = sb("big_b", [P, H, P])
        state = sb("state", [P, B, H, HV])
        run_max = sb("run_max", [P, B, H])
        ctx_s = sb("ctx_s", [P, KC, P])
        kt_s = sb("kt_s", [P, KC, P])
        q_now = sb("q_now", [P, KC, T])
        v_s = sb("v_s", [P, B, H, HV])
        bv_b = sb("bv_b", [P, D])
        bo_b = sb("bo_b", [P, D])
        sbv_b = sb("sbv_b", [P, D])
        sbo_b = sb("sbo_b", [P, D])
        cols = sb("cols", [P, 4, KC])
        gate_s = sb("gate_s", [P, KC, E])
        ident = sb("ident", [P, P])
        bias3 = sb("bias3", [P, P], BF16)
        ones3 = sb("ones3", [P, P], BF16)
        mc = sb("mc", [P, H])
        mnew = sb("mnew", [P, H])
        negm = sb("negm", [P, H])
        mdiff = sb("mdiff", [P, H])
        alpha = sb("alpha", [P, H])
        norm_c = sb("norm_c", [P, B, H])
        stats = sb("stats", [P, B, 6])
        aggr = sb("aggr", [P, B, 2])
        rstd = sb("rstd", [P, B])
        minus_half = sb("minus_half", [P, B])
        mask_s = sb("mask_s", [NJ, P], U8)
        kb_s = sb("kb_s", [NJ, P])
        kb_m = sb("kb_m", [NJ, P])
        kb_3 = sb("kb_3", [NJ, 3, P], BF16)
        idx = sb("idx", [NJ, 8])
        tri = sb("tri", [NJ, NJ])
        slots = sb("slots", [NJ, NJ + 1])
        pick = sb("pick", [NJ, NJ + 1])
        table = sb("table", [1, 2 * (NJ + 1) + 1], I32)
        gsm = sb("gsm", [P, 4, B * E])
        gred = sb("gred", [P, 4, B])
        prob_t = ctx_s[0:B * E, 0]
        work = ctx_s[0:B * E, 1:3]
        top8 = sb("top8", [B * E, 8])
        chosen = kt_s[0:B * E, 0:3]
        slot_t = sb("slot_t", [P, B * E])
        iota_s = sb("iota_s", [P, CAP])
        onehot = big_b[:].rearrange("p h k -> p (h k)")[:, 0:B * E * CAP].rearrange("p (b e s) -> p b e s", b=B, e=E)
        weighted = big_a[:].rearrange("p h k -> p (h k)")[:, 0:B * E * CAP].rearrange("p (e b s) -> p e b s", b=B, e=E)
        xin = qk[:].rearrange("p i b k t -> p (i b k t)").rearrange("p (k e n) -> p k e n", k=KC, e=E)
        spare = state[:].rearrange("p b h d -> p (b h d)")
        back = spare[:, 0:E * T].rearrange("p (e t) -> p e t", e=E)
        y_s = spare[:, E * T:E * T + 2 * D].rearrange("p (i n) -> p i n", i=2)
        back_now = sb("back_now", [P, 2, T])
        h_s = tr[:].rearrange("p k n -> p (k n)").rearrange("p (c n) -> p c n", c=FC)
        rounded = big_b[:].rearrange("p h k -> p (h k)").bitcast(BF16)[:, 0:B * D].rearrange("p (b n) -> p b n", b=B)

        ps = ctx.enter_context(nc.psum_tensor("ps", [P, 4, 512], F32))
        pk = ctx.enter_context(nc.psum_tensor("pk", [P, 512], F32))
        pv = ctx.enter_context(nc.psum_tensor("pv", [P, 512], F32))
        po = ctx.enter_context(nc.psum_tensor("po", [P, 2, 512], F32))
        banks = [ps[:, 0], ps[:, 1], ps[:, 2], ps[:, 3], pk[:], pv[:], po[:, 0], po[:, 1]]

        rows3 = nc.dram_tensor("rows3", [NJ, 3, P], BF16, kind="Internal").ap()

        in_mask, in_x, in_kv, in_q, in_o, in_s, in_gate, in_cols = (sem(f"in_{n}") for n in (
            "mask", "x", "kv", "q", "o", "s", "gate", "cols"))
        rows_out = sem("rows_out")
        consts = sem("consts")
        act_ok = sem("act_ok"); place_mm = sem("place_mm"); place_ok = sem("place_ok")
        pick_ok = sem("pick_ok"); table_mm = sem("table_mm"); table_ok = sem("table_ok"); rows_ok = sem("rows_ok")
        ctx_in = sem("ctx_in"); bias_in = sem("bias_in"); k_mm = sem("k_mm"); v_mm = sem("v_mm")
        k_out = sem("k_out"); v_out = sem("v_out"); s_mm = sem("s_mm"); q_staged = sem("q_staged")
        negm_ok = sem("negm_ok"); alpha_ok = sem("alpha_ok"); p_ok = sem("p_ok"); pt_mm = sem("pt_mm")
        pt_dve = sem("pt_dve"); pt_act = sem("pt_act"); pv_mm = sem("pv_mm"); summed = sem("summed")
        loop_dve = sem("loop_dve")
        var_ok = sem("var_ok"); rstd_ok = sem("rstd_ok")
        dchain = sem("dchain"); pchain = sem("pchain")
        normed = [sem(f"normed{i}") for i in range(5)]
        tr_mm = [sem(f"tr_mm{i}") for i in range(5)]
        tr_dve = [sem(f"tr_dve{i}") for i in range(5)]
        tr_act = [sem(f"tr_act{i}") for i in range(5)]
        q_mm = sem("q_mm"); q_out = sem("q_out")
        o_mm = sem("o_mm"); o_out = sem("o_out")
        q2_mm = sem("q2_mm"); k2_mm = sem("k2_mm"); v2_mm = sem("v2_mm")
        q2_act = sem("q2_act"); q2_out = sem("q2_out"); k2_out = sem("k2_out"); v2_out = sem("v2_out")
        s2_mm = sem("s2_mm"); s2_clamped = sem("s2_clamped"); e2_ok = sem("e2_ok"); pv2_mm = sem("pv2_mm"); pv2_out = sem("pv2_out")
        o2_mm = sem("o2_mm"); o2_out = sem("o2_out")
        g_mm = sem("g_mm"); g_sub = sem("g_sub"); g_exp = sem("g_exp"); g_ok = sem("g_ok"); pt_g = sem("pt_g")
        slot_ok = sem("slot_ok"); slot_mm = sem("slot_mm"); onehot_ok = sem("onehot_ok"); weighted_ok = sem("weighted_ok")
        xin_mm = sem("xin_mm"); xin_dve = sem("xin_dve"); xin_act = sem("xin_act")
        back_mm = sem("back_mm"); back_ok = sem("back_ok")
        a_in = sem("a_in"); b_in = sem("b_in")
        h_mm = sem("h_mm"); h_ok = sem("h_ok"); y_mm = sem("y_mm"); y_ok = sem("y_ok")
        staged = sem("staged"); sc_mm = sem("sc_mm")
        rounded_ok = sem("rounded_ok"); res_ok = sem("res_ok"); stored = sem("stored")

        def chunk_j(eng, t):
            return eng.value_load(table[0:1, bass.ds(t, 1)], min_val=0, max_val=NJ - 1)

        def chunk_b(eng, t):
            return eng.value_load(table[0:1, bass.ds(t + (NJ + 1), 1)], min_val=0, max_val=B - 1)

        def last_chunk(eng):
            eng.wait_ge(table_ok, 2)
            return eng.value_load(table[0:1, 2 * (NJ + 1):2 * (NJ + 1) + 1], min_val=B - 1, max_val=NJ - 1)

        def prime(eng, *sems):
            for s in sems:
                eng.sem_inc(s, 1)

        block = ctx.enter_context(nc.Block())

        @block.sync
        def _(sp):
            sp.dma_start(mask_s[:], key_mask).then_inc(in_mask, 16)
            sp.dma_start(kb_s[:], key_bias).then_inc(in_mask, 16)
            sp.dma_start(x_s[:], x.rearrange("b t d -> t b d")).then_inc(in_x, 16)
            sp.dma_start(wk_s, wk.rearrange("(k p) n -> p k n", p=P)).then_inc(in_kv, 16)
            sp.dma_start(wv_s, wv.rearrange("(k p) n -> p k n", p=P)).then_inc(in_kv, 16)
            for i, v in enumerate((bq, bk, sbq, sbk)):
                sp.dma_start(cols[:, i, :], v).then_inc(in_cols, 16)
            sp.dma_start(bv_b[:], bv.partition_broadcast(P)).then_inc(in_cols, 16)
            sp.dma_start(wq_s, wq.rearrange("(k p) n -> p k n", p=P)).then_inc(in_q, 16)
            sp.wait_ge(rows_ok, 1)
            sp.dma_start(rows3, kb_3[:]).then_inc(rows_out, 16)
            last = last_chunk(sp)
            sp.wait_ge(rows_out, 16)
            sp.wait_ge(consts, 6)
            with sp.Fori(0, last + 1) as t:
                j = chunk_j(sp, t)
                sp.wait_ge(v_mm, t + 1)
                sp.dma_start(ctx_s[:], ctx_t[bass.ds(j, 1)].rearrange("a p k n -> (a p) k n")).then_inc(ctx_in, 16)
                sp.wait_ge(s_mm, t + 1)
                sp.dma_start(bias3[0:3, :], rows3[bass.ds(j, 1)].rearrange("a r n -> (a r) n")).then_inc(bias_in, 16)
            sp.dma_start(wo_s, wo.rearrange("(k p) n -> p k n", p=P)).then_inc(in_o, 16)
            sp.dma_start(bo_b[:], bo.partition_broadcast(P)).then_inc(in_o, 16)
            for w, s in ((sq, sq_s), (sk, sk_s), (sv, sv_s), (so, so_s)):
                sp.dma_start(s, w.rearrange("(k p) n -> p k n", p=P)).then_inc(in_s, 16)
            sp.dma_start(sbv_b[:], sbv.partition_broadcast(P)).then_inc(in_s, 16)
            sp.dma_start(sbo_b[:], sbo.partition_broadcast(P)).then_inc(in_s, 16)
            sp.dma_start(gate_s[:], gate.rearrange("(k p) e -> p k e", p=P)).then_inc(in_gate, 16)
            sp.wait_ge(o2_mm, B)
            sp.dma_start(w1_s[1], w1[1].rearrange("(k p) f -> p k f", p=P)).then_inc(b_in, 16)
            sp.dma_start(w2_s[1], w2[1].rearrange("(c p) n -> p c n", p=P)).then_inc(b_in, 16)
            with sp.Fori(1, E // 2) as half_e:
                e = half_e * 2
                for par, landed in ((0, a_in), (1, b_in)):
                    sp.wait_ge(h_mm, (e + (par - 1)) * 4)
                    sp.dma_start(w1_s[par], w1[bass.ds(e + par, 1)].rearrange("a (k p) f -> p (a k) f", p=P)).then_inc(landed, 16)
                    sp.wait_ge(y_mm, e + par)
                    sp.dma_start(w2_s[par], w2[bass.ds(e + par, 1)].rearrange("a (c p) n -> p (a c) n", p=P)).then_inc(landed, 16)
            for b in range(B):
                sp.wait_ge(res_ok, b + 1)
                sp.dma_start(out[b], x_s[:, b]).then_inc(stored, 16)
            sp.wait_ge(stored, 16 * B)

        @block.gpsimd
        def _(pool):
            g = nc.gpsimd
            def inverse_roots(i):
                pool.wait_ge(var_ok, i + 1)
                g.tensor_tensor(rstd[:], rstd[:], minus_half[:], ALU.pow).then_inc(rstd_ok, 1)

            g.memset(ident[:], 0.0).then_inc(pchain, 1)
            g.memset(minus_half[:], -0.5).then_inc(pchain, 1)
            g.memset(tri[:], 1.0).then_inc(pchain, 1)
            g.memset(ones3[:], 0.0).then_inc(pchain, 1)
            g.iota(idx[:, 0:1], pattern=[[0, 1]], base=0, channel_multiplier=1,
                   allow_small_or_imprecise_dtypes=True).then_inc(consts, 1)
            g.iota(slots[:], pattern=[[1, NJ + 1]], base=0, channel_multiplier=0,
                   allow_small_or_imprecise_dtypes=True).then_inc(consts, 1)
            g.iota(iota_s[:], pattern=[[1, CAP]], base=1, channel_multiplier=0,
                   allow_small_or_imprecise_dtypes=True).then_inc(consts, 1)
            pool.wait_ge(pchain, 4)
            g.affine_select(out=ident[:], in_=ident[:], compare_op=ALU.not_equal, fill=1.0, base=0,
                            pattern=[[-1, P]], channel_multiplier=1).then_inc(consts, 1)
            g.affine_select(out=tri[:], in_=tri[:], compare_op=ALU.is_gt, fill=0.0, base=0,
                            pattern=[[1, NJ]], channel_multiplier=-1).then_inc(consts, 1)
            g.memset(bias3[:], 0.0).then_inc(consts, 1)
            g.memset(ones3[0:3, :], 1.0).then_inc(consts, 1)
            g.memset(idx[:, 5:6], 1.0).then_inc(consts, 1)
            g.memset(v_s[:, :, :, DH:HV], 1.0).then_inc(consts, 1)
            g.memset(state[:], 0.0).then_inc(consts, 1)
            g.memset(run_max[:], -MASKED).then_inc(consts, 1)
            inverse_roots(0)
            last = last_chunk(pool)
            pool.wait_ge(q_out, 4)
            with pool.Fori(0, last + 1) as t:
                b = chunk_b(pool, t)
                pool.wait_ge(s_mm, t + 1)
                g.tensor_copy(q_now[:], qt[:, bass.ds(b, 1)].rearrange("p a k n -> p (a k) n")).then_inc(q_staged, 1)
            inverse_roots(1)
            inverse_roots(2)
            pool.wait_ge(back_ok, 2)
            for par in range(2):
                g.tensor_copy(back_now[:, par, :], back[:, par, :]).then_inc(staged, 1)
            with pool.Fori(1, E // 2) as half_e:
                e = half_e * 2
                for par in range(2):
                    pool.wait_ge(sc_mm, e + (par - 1))
                    g.tensor_copy(back_now[:, par, :], back[:, bass.ds(e + par, 1), :].rearrange("p a n -> p (a n)")).then_inc(staged, 1)

        @block.scalar
        def _(act):
            a = nc.scalar
            prime(act, pt_act)
            act.dma_start(w1_s[0], w1[0].rearrange("(k p) f -> p k f", p=P)).then_inc(a_in, 16)
            act.dma_start(w2_s[0], w2[0].rearrange("(c p) n -> p c n", p=P)).then_inc(a_in, 16)

            def transposed(i):
                for c in (1, 3):
                    act.wait_ge(tr_mm[i], c + 1)
                    a.copy(tr[:, c], ps[:, c]).then_inc(tr_act[i], 1)

            def k_evacuate(t):
                act.wait_ge(k_mm, t + 1)
                for c in range(KC):
                    ins = a.activation(kt_s[:, c], pk[:, c * P:(c + 1) * P], ACT.Identity, bias=cols[:, 1, c:c + 1])
                ins.then_inc(k_out, 1)

            def softmax_chunk(t, more):
                act.wait_ge(negm_ok, 2 * t + 2)
                act.wait_ge(summed, t + 1)
                a.activation(alpha[:], mdiff[:], ACT.Exp).then_inc(alpha_ok, 1)
                for c in range(STRIPS):
                    for g in range(KC):
                        h = c * KC + g
                        ins = a.activation(big_a[:, h], ps[:, c, g * P:(g + 1) * P], ACT.Exp, bias=negm[:, h:h + 1])
                    ins.then_inc(p_ok, 1)
                if more:
                    k_evacuate(t + 1)
                act.wait_ge(pt_mm, 4 * t + 4)
                a.copy(big_b[:, 3 * KC:4 * KC].rearrange("p h k -> p (h k)"), ps[:, 3]).then_inc(pt_act, 1)

            transposed(0)
            last = last_chunk(act)
            act.wait_ge(in_cols, 80)
            k_evacuate(0)
            with act.Fori(0, last) as t:
                softmax_chunk(t, True)
            softmax_chunk(last, False)
            transposed(1)
            transposed(2)
            for c in range(KC):
                act.wait_ge(q2_mm, c + 1)
                a.activation(qt[:, :, c], ps[:, c].rearrange("p (b t) -> p b t", b=B), ACT.Identity,
                             bias=cols[:, 2, c:c + 1]).then_inc(q2_act, 1)
            for c in range(KC):
                act.wait_ge(k2_mm, c + 1)
                a.activation(kt2[:, :, c], banks[4 + c].rearrange("p (b t) -> p b t", b=B), ACT.Identity,
                             bias=cols[:, 3, c:c + 1]).then_inc(q2_act, 1)
            for u in range(2 * B):
                half = big_a if u % 2 == 0 else big_b
                act.wait_ge(s2_clamped, u + 1)
                a.activation(half[:, 8:16], half[:, 0:8], ACT.Exp).then_inc(e2_ok, 1)
            transposed(3)
            transposed(4)
            act.wait_ge(g_sub, 1)
            a.activation(gsm[:, 2], gsm[:, 1], ACT.Exp).then_inc(g_exp, 1)
            for i in range(4):
                c = 2 * i + 1
                act.wait_ge(xin_mm, c + 1)
                a.copy(xin[:, c % 4].rearrange("p e (b s) -> p b e s", b=B)[:, 2 * (c // 4):2 * (c // 4) + 2],
                       banks[c].rearrange("p (b e s) -> p b e s", b=2, e=E)).then_inc(xin_act, 1)
            with act.Fori(0, E) as e:
                for q in range(4):
                    act.wait_ge(h_mm, e * 4 + q + 1)
                    act.wait_ge(y_mm, e + 1)
                    a.activation(h_s[:, 4 * q:4 * q + 4].rearrange("p c n -> p (c n)"), (pk, pv)[q % 2][:],
                                 ACT.Gelu_apprx_tanh).then_inc(h_ok, 1)

        @block.vector
        def _(dve):
            v = nc.vector
            links = [0]
            ln_count = [0]

            def link(ins):
                ins.then_inc(dchain, 1)
                links[0] += 1
                dve.wait_ge(dchain, links[0])

            def layer_norm(i):
                for b in range(B):
                    ins = v.bn_stats(stats[:, b], x_s[:, b])
                link(ins)
                for b in range(B):
                    ins = v.bn_aggr(aggr[:, b], stats[:, b])
                link(ins)
                v.tensor_scalar(rstd[:], aggr[:, :, 1], EPS_LN, None, ALU.add).then_inc(var_ok, 1)
                ln_count[0] += 1
                dve.wait_ge(rstd_ok, ln_count[0])
                for b in range(B):
                    v.tensor_scalar(norm[:, b], x_s[:, b], aggr[:, b, 0:1], rstd[:, b:b + 1],
                                    ALU.subtract, ALU.mult).then_inc(normed[i], 1)

            def transposed(i):
                for c in (0, 2):
                    dve.wait_ge(tr_mm[i], c + 1)
                    v.tensor_copy(tr[:, c], ps[:, c]).then_inc(tr_dve[i], 1)

            def heads(ap):
                return ap.rearrange("p (g j d) -> p j g d", j=STRIPS, d=DH)

            prime(dve, summed, pt_dve)
            dve.wait_ge(in_mask, 32)
            dve.wait_ge(consts, 11)
            v.tensor_reduce(idx[:, 3:4], mask_s[:], AX.X, ALU.max)
            link(v.tensor_scalar(idx[:, 2:3], idx[:, 0:1], float(NCH), None, ALU.is_ge))
            for b in range(2, B):
                link(v.scalar_tensor_tensor(idx[:, 2:3], idx[:, 0:1], float(b * NCH), idx[:, 2:3], ALU.is_ge, ALU.add))
            link(v.scalar_tensor_tensor(idx[:, 1:2], idx[:, 2:3], -float(NCH), idx[:, 0:1], ALU.mult, ALU.add))
            link(v.tensor_scalar(idx[:, 6:7], idx[:, 1:2], float(NCH - 1), None, ALU.is_equal))
            v.tensor_tensor(idx[:, 7:8], idx[:, 3:4], idx[:, 6:7], ALU.max).then_inc(act_ok, 1)
            link(v.tensor_scalar(kb_m[:], mask_s[:], 1.0, MASKED, ALU.subtract, ALU.mult))
            link(v.tensor_tensor(kb_m[:], kb_m[:], kb_s[:], ALU.add))
            link(v.tensor_copy(kb_3[:, 0], kb_m[:]))
            link(v.tensor_tensor(kb_m[:], kb_m[:], kb_3[:, 0], ALU.subtract))
            link(v.tensor_copy(kb_3[:, 1], kb_m[:]))
            link(v.tensor_tensor(kb_m[:], kb_m[:], kb_3[:, 1], ALU.subtract))
            v.tensor_copy(kb_3[:, 2], kb_m[:]).then_inc(rows_ok, 1)
            dve.wait_ge(place_mm, 1)
            link(v.tensor_copy(idx[:, 4:5], pv[0:NJ, 0:1]))
            v.tensor_scalar(pick[:], slots[:], idx[:, 4:5], idx[:, 7:8], ALU.is_equal, ALU.mult).then_inc(pick_ok, 1)
            dve.wait_ge(table_mm, 1)
            n_at = 2 * (NJ + 1)
            v.tensor_copy(table[:, 0:n_at], pv[0:1, 0:n_at]).then_inc(table_ok, 1)
            v.tensor_scalar(table[:, n_at:n_at + 1], pv[0:1, n_at:n_at + 1], -1.0, None, ALU.add).then_inc(table_ok, 1)

            dve.wait_ge(in_x, 16)
            layer_norm(0)
            transposed(0)
            dve.wait_ge(in_cols, 80)
            for c in range(KC):
                dve.wait_ge(q_mm, c + 1)
                v.tensor_scalar(qt[:, :, c], ps[:, c].rearrange("p (b t) -> p b t", b=B), cols[:, 0, c:c + 1],
                                SCALE, ALU.add, ALU.mult).then_inc(q_out, 1)

            def v_evacuate(t):
                dve.wait_ge(v_mm, t + 2)
                v.tensor_tensor(v_s[:, 0].rearrange("p (j g) d -> p j g d", j=STRIPS)[:, :, :, 0:DH],
                                heads(pv[:]), heads(bv_b[:]), ALU.add).then_inc(v_out, 1)

            def softmax_chunk(t, more):
                b = chunk_b(dve, t)
                rm = run_max[:, bass.ds(b, 1)].rearrange("p a h -> p (a h)")
                st = state[:, bass.ds(b, 1)].rearrange("p a h d -> p (a h) d")
                dve.wait_ge(s_mm, t + 2)
                v.tensor_reduce(mc[:], ps[:].rearrange("p c (g k) -> p (c g) k", k=P), AX.X, ALU.max).then_inc(loop_dve, 1)
                dve.wait_ge(loop_dve, 4 * t + 1)
                v.tensor_tensor(mnew[:], mc[:], rm, ALU.max).then_inc(loop_dve, 1)
                dve.wait_ge(loop_dve, 4 * t + 2)
                v.tensor_scalar(negm[:], mnew[:], -1.0, None, ALU.mult).then_inc(negm_ok, 1)
                v.tensor_tensor(mdiff[:], rm, mnew[:], ALU.subtract).then_inc(negm_ok, 1)
                dve.wait_ge(negm_ok, 2 * t + 2)
                v.tensor_tensor(rm, mc[:], rm, ALU.max).then_inc(loop_dve, 1)
                dve.wait_ge(alpha_ok, t + 1)
                v.tensor_tensor(st, st, alpha[:].unsqueeze(2).broadcast_to([P, H, HV]), ALU.mult).then_inc(loop_dve, 1)
                for c in range(3):
                    dve.wait_ge(pt_mm, 4 * t + c + 1)
                    v.tensor_copy(big_b[:, c * KC:(c + 1) * KC].rearrange("p h k -> p (h k)"), ps[:, c]).then_inc(pt_dve, 1)
                dve.wait_ge(pv_mm, t + 1)
                dve.wait_ge(loop_dve, 4 * t + 4)
                for c in range(2):
                    half = st[:, 8 * c:8 * c + 8]
                    ins = v.tensor_tensor(half, half, po[:, c, 0:8 * HV].rearrange("p (h d) -> p h d", d=HV), ALU.add)
                ins.then_inc(summed, 1)
                if more:
                    v_evacuate(t + 1)

            last = last_chunk(dve)
            v_evacuate(0)
            with dve.Fori(0, last) as t:
                softmax_chunk(t, True)
            softmax_chunk(last, False)

            dve.wait_ge(summed, last + 2)
            link(v.tensor_scalar(norm_c[:], run_max[:], -0.1 * MASKED, None, ALU.is_gt))
            link(v.tensor_tensor(run_max[:], norm_c[:], state[:, :, :, DH], ALU.mult))
            link(v.reciprocal(run_max[:], run_max[:]))
            link(v.tensor_tensor(norm_c[:], norm_c[:], run_max[:], ALU.mult))
            for b in range(B):
                v.tensor_tensor(heads(norm[:, b]), state[:, b].rearrange("p (j g) d -> p j g d", j=STRIPS)[:, :, :, 0:DH],
                                norm_c[:, b].rearrange("p (j g) -> p j g", j=STRIPS).unsqueeze(3).broadcast_to([P, STRIPS, KC, DH]),
                                ALU.mult).then_inc(normed[1], 1)
            dve.wait_ge(in_o, 32)
            for b in range(B):
                ins = v.tensor_tensor(x_s[:, b], x_s[:, b], bo_b[:], ALU.add)
            link(ins)
            transposed(1)
            for b in range(B):
                dve.wait_ge(o_mm, b + 1)
                ins = v.tensor_tensor(x_s[:, b], x_s[:, b], ps[:, b], ALU.add)
                ins.then_inc(o_out, 1)
            dve.wait_ge(o_out, B)
            layer_norm(2)
            transposed(2)
            for c in range(KC):
                dve.wait_ge(q2_act, c + 1)
                link(v.tensor_scalar(qt[:, :, c], qt[:, :, c], SCALE, LO, ALU.mult, ALU.max))
                v.tensor_scalar(qt[:, :, c], qt[:, :, c], HI, None, ALU.min).then_inc(q2_out, 1)
            for c in range(KC):
                dve.wait_ge(q2_act, KC + c + 1)
                v.tensor_scalar(kt2[:, :, c], kt2[:, :, c], LO, HI, ALU.max, ALU.min).then_inc(k2_out, 1)
            dve.wait_ge(in_s, 96)
            for b in range(B):
                dve.wait_ge(v2_mm, b + 1)
                dst = v_s[:, b].rearrange("p (j g) d -> p j g d", j=STRIPS)[:, :, :, 0:DH]
                link(v.tensor_tensor(dst, heads(ps[:, b]), heads(sbv_b[:]), ALU.add))
                v.tensor_scalar(dst, dst, LO, HI, ALU.max, ALU.min).then_inc(v2_out, 1)

            def clamp_scores(u):
                half = big_a if u % 2 == 0 else big_b
                dve.wait_ge(s2_mm, u + 1)
                v.tensor_scalar(half[:, 0:8].rearrange("p h k -> p (h k)"),
                                ps[:, 2 * (u % 2):2 * (u % 2) + 2].rearrange("p c n -> p (c n)"),
                                LO, HI, ALU.max, ALU.min).then_inc(s2_clamped, 1)

            def normalise(u):
                b, c = u // 2, u % 2
                o3 = po[:, c, 0:8 * HV].rearrange("p (h d) -> p h d", d=HV)
                dve.wait_ge(pv2_mm, u + 1)
                if u:
                    dve.wait_ge(pv2_out, u)
                link(v.reciprocal(mc[:, 0:8], o3[:, :, DH]))
                dst = heads(norm[:, b])[:, 2 * c:2 * c + 2]
                ins = v.tensor_tensor(dst, o3[:, :, 0:DH].rearrange("p (j g) d -> p j g d", j=2),
                                      mc[:, 0:8].rearrange("p (j g) -> p j g", j=2).unsqueeze(3).broadcast_to([P, 2, KC, DH]),
                                      ALU.mult)
                ins.then_inc(pv2_out, 1)
                if c == 1:
                    dve.wait_ge(pv2_out, u + 1)
                    v.tensor_scalar(norm[:, b], norm[:, b], LO, HI, ALU.max, ALU.min).then_inc(normed[3], 1)

            clamp_scores(0)
            for u in range(2 * B):
                if u + 1 < 2 * B:
                    clamp_scores(u + 1)
                normalise(u)
            transposed(3)
            for b in range(B):
                dve.wait_ge(o2_mm, b + 1)
                link(v.tensor_tensor(norm[:, b], ps[:, b], sbo_b[:], ALU.add))
                link(v.tensor_scalar(norm[:, b], norm[:, b], LO, HI, ALU.max, ALU.min))
                ins = v.tensor_tensor(x_s[:, b], x_s[:, b], norm[:, b], ALU.add)
            link(ins)
            layer_norm(4)
            transposed(4)

            def by_batch(i):
                return gsm[:, i].rearrange("p (b e) -> p b e", b=B)

            def wide(i):
                return gred[:, i].unsqueeze(2).broadcast_to([P, B, E])

            g_psum = pk[:, 0:B * E].rearrange("p (b e) -> p b e", b=B)
            dve.wait_ge(g_mm, 1)
            link(v.tensor_reduce(gred[:, 0], g_psum, AX.X, ALU.max))
            v.tensor_tensor(by_batch(1), g_psum, wide(0), ALU.subtract).then_inc(g_sub, 1)
            dve.wait_ge(g_exp, 1)
            link(v.tensor_reduce(gred[:, 1], by_batch(2), AX.X, ALU.add))
            link(v.reciprocal(gred[:, 2], gred[:, 1]))
            v.tensor_tensor(by_batch(3), by_batch(2), wide(2), ALU.mult).then_inc(g_ok, 1)
            dve.wait_ge(pt_g, 1)
            link(v.tensor_copy(prob_t, pv[0:B * E, 0:T]))
            src = prob_t
            for r in range(CAP // 8):
                link(v.max(top8[:], src))
                link(v.match_replace(work[:, r % 2], top8[:], src, -1.0))
                src = work[:, r % 2]
            link(v.tensor_scalar(chosen[:, 0], src, 0.0, None, ALU.is_lt))
            link(v.memset(chosen[:, 2], 0.0))
            link(v.tensor_tensor_scan(chosen[:, 1], chosen[:, 0], chosen[:, 2], 0.0, ALU.add, ALU.add))
            v.tensor_tensor(chosen[:, 2], chosen[:, 0], chosen[:, 1], ALU.mult).then_inc(slot_ok, 1)
            dve.wait_ge(slot_mm, 1)
            link(v.tensor_copy(slot_t[:], pk[:, 0:B * E]))
            be = "p b e s -> p (b e) s"
            v.tensor_tensor(onehot.rearrange(be), slot_t[:].unsqueeze(2).broadcast_to([P, B * E, CAP]),
                            iota_s[:].unsqueeze(1).broadcast_to([P, B * E, CAP]), ALU.is_equal).then_inc(onehot_ok, 1)
            dve.wait_ge(onehot_ok, 1)
            v.tensor_tensor(weighted.rearrange("p e b s -> p b e s"), onehot,
                            by_batch(3).unsqueeze(3).broadcast_to([P, B, E, CAP]), ALU.mult).then_inc(weighted_ok, 1)
            for i in range(4):
                c = 2 * i
                dve.wait_ge(xin_mm, c + 1)
                v.tensor_copy(xin[:, c % 4].rearrange("p e (b s) -> p b e s", b=B)[:, 2 * (c // 4):2 * (c // 4) + 2],
                              banks[c].rearrange("p (b e s) -> p b e s", b=2, e=E)).then_inc(xin_dve, 1)
            for i in range(2):
                dve.wait_ge(back_mm, i + 1)
                v.tensor_copy(back[:, 4 * i:4 * i + 4].rearrange("p e t -> p (e t)"), (pk, pv)[i][:]).then_inc(back_ok, 1)
            for par in range(2):
                dve.wait_ge(y_mm, par + 2)
                v.tensor_copy(y_s[:, par], po[:, par]).then_inc(y_ok, 1)
            with dve.Fori(1, E // 2) as half_e:
                e = half_e * 2
                for par in range(2):
                    dve.wait_ge(y_mm, e + (par + 2))
                    dve.wait_ge(sc_mm, e + (par - 1))
                    v.tensor_copy(y_s[:, par], po[:, par]).then_inc(y_ok, 1)
            dve.wait_ge(sc_mm, E)
            for b in range(B):
                v.tensor_copy(rounded[:, b], ps[:, b]).then_inc(rounded_ok, 1)
                dve.wait_ge(rounded_ok, b + 1)
                v.tensor_tensor(x_s[:, b], x_s[:, b], rounded[:, b], ALU.add).then_inc(res_ok, 1)

        @block.tensor
        def _(pe):
            mm = nc.tensor.matmul

            def k_project(t):
                pe.wait_ge(ctx_in, t * 16 + 16)
                if not isinstance(t, int):
                    pe.wait_ge(k_out, t)
                for g in range(KC):
                    for k in range(KC):
                        ins = mm(pk[:, g * P:(g + 1) * P], wk_s[:, k, g * P:(g + 1) * P], ctx_s[:, k], start=k == 0, stop=k == KC - 1)
                ins.then_inc(k_mm, 1)

            def v_project(t):
                if not isinstance(t, int):
                    pe.wait_ge(v_out, t)
                for k in range(KC):
                    ins = mm(pv[:], ctx_s[:, k], wv_s[:, k], start=k == 0, stop=k == KC - 1)
                ins.then_inc(v_mm, 1)

            def transpose_all(i):
                pe.wait_ge(normed[i], B)
                for c in range(KC):
                    for b in range(B):
                        ins = nc.tensor.transpose(ps[:, c, b * T:(b + 1) * T], norm[:, b, c * P:(c + 1) * P], ident[:])
                    ins.then_inc(tr_mm[i], 1)

            def transposed(i):
                pe.wait_ge(tr_dve[i], 2)
                pe.wait_ge(tr_act[i], 2)

            def project_t(w, dst, done):
                for g in range(KC):
                    for k in range(KC):
                        ins = mm(dst[g], w[:, k, g * P:(g + 1) * P], tr[:, k], start=k == 0, stop=k == KC - 1)
                    ins.then_inc(done, 1)

            def project(w, dst, done):
                for b in range(B):
                    for k in range(KC):
                        ins = mm(dst[b], tr[:, k, b * T:(b + 1) * T], w[:, k], start=k == 0, stop=k == KC - 1)
                    ins.then_inc(done, 1)

            prime(pe, v_mm, s_mm, y_mm)
            pe.wait_ge(consts, 11)
            pe.wait_ge(act_ok, 1)
            mm(pv[0:NJ, 0:1], tri[:], idx[:, 7:8], start=True, stop=True).then_inc(place_mm, 1)
            pe.wait_ge(pick_ok, 1)
            mm(pv[0:1, 0:NJ + 1], idx[:, 0:1], pick[:], start=True, stop=True)
            mm(pv[0:1, NJ + 1:2 * (NJ + 1)], idx[:, 2:3], pick[:], start=True, stop=True)
            mm(pv[0:1, 2 * (NJ + 1):2 * (NJ + 1) + 1], idx[:, 7:8], idx[:, 5:6], start=True, stop=True).then_inc(table_mm, 1)
            last = last_chunk(pe)
            transpose_all(0)
            transposed(0)
            pe.wait_ge(in_q, 16)
            project_t(wq_s, banks[0:4], q_mm)

            def scores(t):
                pe.wait_ge(bias_in, t * 16 + 16)
                pe.wait_ge(q_staged, t + 1)
                pe.wait_ge(k_out, t + 1)
                pe.wait_ge(pt_dve, t * 3 + 1)
                pe.wait_ge(pt_act, t + 1)
                for c in range(STRIPS):
                    mm(ps[:, c].rearrange("p (g k) -> p g k", g=KC), ones3[:], bias3[:].unsqueeze(1).broadcast_to([P, KC, P]),
                       start=True, stop=False, skip_group_check=True)
                for g in range(KC):
                    for c in range(STRIPS):
                        r = slice(c * DH, (c + 1) * DH)
                        ins = mm(ps[:, c, g * P:(g + 1) * P], q_now[r, g], kt_s[r, g], start=False, stop=True, skip_group_check=True)
                ins.then_inc(s_mm, 1)

            def values(t):
                for c in range(STRIPS):
                    pe.wait_ge(p_ok, t * 4 + (c + 1))
                    for g in range(KC):
                        ins = nc.tensor.transpose(ps[:, c, g * P:(g + 1) * P], big_a[:, c * KC + g], ident[:])
                    ins.then_inc(pt_mm, 1)
                pe.wait_ge(v_out, t + 1)
                pe.wait_ge(summed, t + 1)
                for h in range(H):
                    if h % KC == 0 and h < 3 * KC:
                        pe.wait_ge(pt_dve, t * 3 + (h // KC + 2))
                    if h == 3 * KC:
                        pe.wait_ge(pt_act, t + 2)
                    ins = mm(po[:, h // 8, (h % 8) * HV:(h % 8 + 1) * HV], big_b[:, h], v_s[:, 0, h], start=True, stop=True)
                ins.then_inc(pv_mm, 1)

            pe.wait_ge(in_kv, 32)
            pe.wait_ge(q_out, 4)
            k_project(0)
            v_project(0)
            with pe.Fori(0, last) as t:
                scores(t)
                k_project(t + 1)
                v_project(t + 1)
                values(t)
            scores(last)
            values(last)

            transpose_all(1)
            transposed(1)
            pe.wait_ge(in_o, 32)
            project(wo_s, banks[0:4], o_mm)
            transpose_all(2)
            transposed(2)
            pe.wait_ge(in_s, 96)
            pe.wait_ge(summed, last + 2)
            project_t(sq_s, banks[0:4], q2_mm)
            project_t(sk_s, banks[4:8], k2_mm)
            pe.wait_ge(q2_act, KC)
            project(sv_s, banks[0:4], v2_mm)

            def scores2(u):
                b, c0 = u // 2, 2 * (u % 2)
                if u == 0:
                    pe.wait_ge(q2_out, KC)
                    pe.wait_ge(k2_out, KC)
                    pe.wait_ge(v2_out, B)
                if u >= 2:
                    pe.wait_ge(s2_clamped, u - 1)
                for g in range(KC):
                    for c in (c0, c0 + 1):
                        r = slice(c * DH, (c + 1) * DH)
                        ins = mm(ps[:, c, g * P:(g + 1) * P], kt2[r, b, g], qt[r, b, g], start=True, stop=True)
                ins.then_inc(s2_mm, 1)

            def values2(u):
                b, c = u // 2, u % 2
                half = big_a if c == 0 else big_b
                pe.wait_ge(e2_ok, u + 1)
                if u >= 2:
                    pe.wait_ge(pv2_out, u - 1)
                for h in range(8):
                    ins = mm(po[:, c, h * HV:(h + 1) * HV], half[:, 8 + h], v_s[:, b, 8 * c + h], start=True, stop=True)
                ins.then_inc(pv2_mm, 1)

            scores2(0)
            for u in range(2 * B):
                if u + 1 < 2 * B:
                    scores2(u + 1)
                values2(u)
            transpose_all(3)
            transposed(3)
            project(so_s, banks[0:4], o2_mm)
            transpose_all(4)
            transposed(4)
            pe.wait_ge(in_gate, 16)
            for b in range(B):
                for k in range(KC):
                    ins = mm(pk[:, b * E:(b + 1) * E], tr[:, k, b * T:(b + 1) * T], gate_s[:, k], start=k == 0, stop=k == KC - 1)
            ins.then_inc(g_mm, 1)
            pe.wait_ge(g_ok, 1)
            nc.tensor.transpose(pv[0:B * E, 0:T], gsm[:, 3], ident[:]).then_inc(pt_g, 1)
            pe.wait_ge(slot_ok, 1)
            nc.tensor.transpose(pk[:, 0:B * E], chosen[:, 2], ident[0:B * E, 0:B * E]).then_inc(slot_mm, 1)
            pe.wait_ge(onehot_ok, 1)
            for c in range(8):
                k, pair = c % 4, c // 4
                for b in (2 * pair, 2 * pair + 1):
                    ins = mm(banks[c][:, (b % 2) * E * CAP:(b % 2 + 1) * E * CAP], norm[:, b, k * P:(k + 1) * P],
                             onehot[:, b].rearrange("p e s -> p (e s)"), start=True, stop=True)
                ins.then_inc(xin_mm, 1)
            pe.wait_ge(weighted_ok, 1)
            pe.wait_ge(xin_dve, 4)
            pe.wait_ge(xin_act, 4)
            for e in range(E):
                ins = nc.tensor.transpose((pk, pv)[e // 4][:, (e % 4) * T:(e % 4 + 1) * T], weighted[:, e].rearrange("p b s -> p (b s)"), ident[:])
                if e % 4 == 3:
                    ins.then_inc(back_mm, 1)
            pe.wait_ge(back_ok, 2)

            def hidden(e, par):
                pe.wait_ge((a_in, b_in)[par], (e - par) * 16 + 32)
                for q in range(4):
                    if q >= 2 or not isinstance(e, int) or e > 0:
                        pe.wait_ge(h_ok, e * 4 + (q - 1))
                    for f in range(4 * q, 4 * q + 4):
                        for k in range(KC):
                            ins = mm((pk, pv)[q % 2][:, (f % 4) * P:(f % 4 + 1) * P], w1_s[par][:, k, f * P:(f + 1) * P],
                                     xin[:, k, bass.ds(e, 1)].rearrange("p a n -> p (a n)"), start=k == 0, stop=k == KC - 1)
                    ins.then_inc(h_mm, 1)

            def expert_out(e, par):
                if not isinstance(e, int) or e >= 2:
                    pe.wait_ge(y_ok, e - 1)
                for f in range(FC):
                    if f % 4 == 0:
                        pe.wait_ge(h_ok, e * 4 + (f // 4 + 1))
                    ins = mm(po[:, par], h_s[:, f], w2_s[par][:, f], start=f == 0, stop=f == FC - 1)
                ins.then_inc(y_mm, 1)

            def scatter(e, par):
                pe.wait_ge(staged, e + 1)
                pe.wait_ge(y_ok, e + 1)
                for b in range(B):
                    r = slice(b * CAP, (b + 1) * CAP)
                    first = isinstance(e, int) and e == 0
                    ins = mm(ps[:, b], back_now[r, par], y_s[r, par], start=first, stop=False, skip_group_check=True)
                ins.then_inc(sc_mm, 1)

            def pair(e, first):
                hidden(e, 0)
                if not first:
                    scatter(e - 1, 1)
                expert_out(e, 0)
                hidden(e + 1, 1)
                scatter(e, 0)
                expert_out(e + 1, 1)

            pair(0, True)
            with pe.Fori(1, E // 2) as half_e:
                e = half_e * 2
                pair(e, False)
            scatter(E - 1, 1)


_INS = ["x", "ctx_t", "key_bias", "key_mask", "wq", "bq", "wk", "bk", "wv", "bv", "wo", "bo",
        "sq", "sbq", "sk", "sbk", "sv", "sbv", "so", "sbo", "gate", "w1", "w2"]


def kernel(**inputs):
    import numpy as np
    import concourse.bacc as bacc
    from concourse.bass_utils import run_bass_kernel_spmd

    a = {k: np.asarray(v) for k, v in inputs.items()}

    def columns(v):
        return v.reshape(KC, P).T

    kv_w, kv_b = a["L0_xattn_Wkv_w"], a["L0_xattn_Wkv_b"]
    laid = {
        "x": a["x"],
        "ctx_t": a["ctx_1024"].reshape(NJ, P, KC, P).transpose(0, 3, 2, 1),
        "key_bias": a["fside_BxS2_0"].reshape(NJ, P),
        "key_mask": a["mask_BxS2_bk0"].reshape(NJ, P),
        "wq": a["L0_xattn_Wq_w"].T, "bq": columns(a["L0_xattn_Wq_b"]),
        "wk": kv_w[:D].T, "bk": columns(kv_b[:D]),
        "wv": kv_w[D:].T, "bv": kv_b[D:],
        "wo": a["L0_xattn_out_w"].T, "bo": a["L0_xattn_out_b"],
        "sq": a["L0_attn_Wq"].T, "sbq": columns(a["L0_attn_bq"]),
        "sk": a["L0_attn_Wk"].T, "sbk": columns(a["L0_attn_bk"]),
        "sv": a["L0_attn_Wv"].T, "sbv": a["L0_attn_bv"],
        "so": a["L0_attn_Wo"].T, "sbo": a["L0_attn_bo"],
        "gate": a["L0_ffn_gate_w"], "w1": a["L0_ffn_w1"], "w2": a["L0_ffn_w2"],
    }
    nc = bacc.Bacc("TRN2", target_bir_lowering=False, num_devices=1, dynamic_dma_scratch_size=1024)
    arrays, args = {}, []
    for name in _INS:
        v = np.ascontiguousarray(laid[name])
        arrays[f"in_{name}"] = v
        args.append(nc.dram_tensor(f"in_{name}", v.shape, mybir.dt.from_np(v.dtype), kind="ExternalInput").ap())
    args.append(nc.dram_tensor("out", (B, T, D), F32, kind="ExternalOutput").ap())
    decoder_layer(nc, *args)
    r = run_bass_kernel_spmd(nc, [arrays], core_ids=[0])
    return r.results[0]["out"]
```

```python
from contextlib import ExitStack

import concourse.bass as bass
from concourse import mybir

ALU = mybir.AluOpType
ACT = mybir.ActivationFunctionType
AX = mybir.AxisListType
F32 = mybir.dt.float32
F32R = mybir.dt.float32r
BF16 = mybir.dt.bfloat16
I32 = mybir.dt.int32
U8 = mybir.dt.uint8

P = 128
B, T, D = 4, 128, 512
SK = 2048
H, DH = 16, 32
KC = D // P
NCH = SK // P
NJ = B * NCH
STRIPS = P // DH
E, F = 8, 2048
CAP = 2 * T // E
FC = F // P
NQ = F // D
SLOTS = 4
HV = DH + 1
MASKED = 1.0e30
EPS_LN = 1e-5
LO, HI = 1e-7, 1.0 - 1e-7
SCALE = DH ** -0.5


def decoder_layer(nc, x, ctx_t, key_bias, key_mask, wq, bq, wk, bk, wv, bv, wo, bo,
                  sq, sbq, sk, sbk, sv, sbv, so, sbo, gate, w1, w2, out):
    with ExitStack() as ctx:
        def sb(name, shape, dt=F32):
            return ctx.enter_context(nc.sbuf_tensor(name, shape, dt))

        def sem(name):
            return ctx.enter_context(nc.semaphore(name))

        att_w = sb("att_w", [P, 8, KC, D])
        wq_s, wk_s, wv_s, wo_s, sq_s, sk_s, sv_s, so_s = (att_w[:, i] for i in range(8))
        q_wide = att_w[:, 6:8].rearrange("p i c (g t) -> p i c g t", g=KC)
        w_hi = sb("w_hi", [P, SLOTS, KC, D], F32R)
        w_lo = sb("w_lo", [P, SLOTS, KC, D], F32R)

        x_s = sb("x_s", [P, B, D])
        norm = sb("norm", [P, B, D])
        gcol = sb("gcol", [P, E])
        qk = sb("qk", [P, 2, B, KC, T])
        qt, kt2 = qk[:, 0], qk[:, 1]
        tr_gate = qt
        state = sb("state", [P, B, H, HV])
        run_max = sb("run_max", [P, B, H])
        cols = sb("cols", [P, 4, KC])
        gate_s = sb("gate_s", [P, KC, E])
        ident = sb("ident", [P, P])
        bias3 = sb("bias3", [P, P], BF16)
        ones3 = sb("ones3", [P, P], BF16)
        mc = sb("mc", [P, H])
        mnew = sb("mnew", [P, H])
        negm = sb("negm", [P, H])
        mdiff = sb("mdiff", [P, H])
        alpha = sb("alpha", [P, H])
        norm_c = sb("norm_c", [P, B, H])
        stats = sb("stats", [P, B, 6])
        aggr = sb("aggr", [P, B, 2])
        rstd = sb("rstd", [P, B])
        minus_half = sb("minus_half", [P, B])
        table = sb("table", [1, 2 * (NJ + 1) + 1], I32)
        gsm = sb("gsm", [P, 4, B * E])
        gred = sb("gred", [P, 4, B])
        top8 = sb("top8", [B * E, 8])
        slot_t = sb("slot_t", [P, B * E])
        iota_s = sb("iota_s", [P, CAP])
        attention = ExitStack()

        def early(name, shape, dt=F32):
            return attention.enter_context(nc.sbuf_tensor(name, shape, dt))

        tr_hi = early("tr_hi", [P, KC, B * T], F32R)
        tr_lo = early("tr_lo", [P, KC, B * T], F32R)
        big_a = early("big_a", [P, H, P])
        ctx_s = early("ctx_s", [P, KC, P])
        kt_s = early("kt_s", [P, KC, P])
        q_now = early("q_now", [P, KC, T])
        values = ExitStack()
        v_s = values.enter_context(nc.sbuf_tensor("v_s", [P, B, H, HV], F32))
        values.close()
        onehot_s = early("onehot_s", [P, B * E * CAP], F32R)
        early("rest_of_v", [P, B * H * HV - B * E * CAP])
        bv_b = early("bv_b", [P, D])
        bo_b = early("bo_b", [P, D])
        start = ExitStack()

        def first(name, shape, dt=F32):
            return start.enter_context(nc.sbuf_tensor(name, shape, dt))

        mask_s = first("mask_s", [NJ, P], U8)
        kb_s = first("kb_s", [NJ, P])
        kb_m = first("kb_m", [NJ, P])
        kb_3 = first("kb_3", [NJ, 3, P], BF16)
        idx = first("idx", [NJ, 8])
        tri = first("tri", [NJ, NJ])
        slots = first("slots", [NJ, NJ + 1])
        pick = first("pick", [NJ, NJ + 1])
        start.close()
        big_b = early("big_b", [P, H, P])
        attention.close()
        x_now = sb("x_now", [P, KC, P])
        xin_hi = sb("xin_hi", [P, KC, P], F32R)
        xin_lo = sb("xin_lo", [P, KC, P], F32R)
        h_s = sb("h_s", [P, 2, D])
        ht_hi = sb("ht_hi", [P, FC, P], F32R)
        ht_lo = sb("ht_lo", [P, FC, P], F32R)
        y_s = sb("y_s", [P, D])
        y_hi = sb("y_hi", [P, D], F32R)
        y_lo = sb("y_lo", [P, D], F32R)
        back_now = sb("back_now", [P, T], F32R)
        rounded = sb("rounded", [P, B, D], BF16)

        prob_t = ctx_s[0:B * E, 0]
        work = ctx_s[0:B * E, 1:3]
        chosen = kt_s[0:B * E, 0:3]
        norm_hi, norm_lo = (t[:].rearrange("p k n -> p (k n)").rearrange("p (b n) -> p b n", b=B) for t in (tr_hi, tr_lo))
        onehot = onehot_s[:].rearrange("p (b e s) -> p b e s", b=B, e=E)
        weighted = big_a[:].rearrange("p h k -> p (h k)")[:, 0:B * E * CAP].rearrange("p (e b s) -> p e b s", b=B, e=E)
        xin = qk[:].rearrange("p i b k t -> p (i b k t)").rearrange("p (k e n) -> p k e n", k=KC, e=E)
        spare = state[:].rearrange("p b h d -> p (b h d)")
        back = spare[:, 0:E * T].rearrange("p (e t) -> p e t", e=E)

        ps = ctx.enter_context(nc.psum_tensor("ps", [P, 4, 512], F32))
        pk = ctx.enter_context(nc.psum_tensor("pk", [P, 512], F32))
        pv = ctx.enter_context(nc.psum_tensor("pv", [P, 512], F32))
        po = ctx.enter_context(nc.psum_tensor("po", [P, 2, 512], F32))
        banks = [ps[:, 0], ps[:, 1], ps[:, 2], ps[:, 3], pk[:], pv[:], po[:, 0], po[:, 1]]

        logits = po[:, 1, 8 * HV:8 * HV + B * E]

        rows3 = nc.dram_tensor("rows3", [NJ, 3, P], BF16, kind="Internal").ap()

        in_mask, in_x, in_wk, in_wv, in_bo, in_sb, in_gate, in_cols = (sem(f"in_{n}") for n in (
            "mask", "x", "wk", "wv", "bo", "sb", "gate", "cols"))
        in_wq, in_wo, in_sq, in_sk, in_sv, in_so = (sem(f"in_{n}") for n in ("wq", "wo", "sq", "sk", "sv", "so"))
        att_hi_ok = sem("att_hi_ok"); att_lo_ok = sem("att_lo_ok")
        rows_out = sem("rows_out")
        consts = sem("consts")
        act_ok = sem("act_ok"); place_mm = sem("place_mm"); place_ok = sem("place_ok")
        pick_ok = sem("pick_ok"); table_mm = sem("table_mm"); table_ok = sem("table_ok"); rows_ok = sem("rows_ok")
        ctx_in = sem("ctx_in"); bias_in = sem("bias_in"); k_mm = sem("k_mm"); v_mm = sem("v_mm")
        k_out = sem("k_out"); v_out = sem("v_out"); s_mm = sem("s_mm"); q_staged = sem("q_staged")
        negm_ok = sem("negm_ok"); alpha_ok = sem("alpha_ok"); p_ok = sem("p_ok"); pt_mm = sem("pt_mm")
        pt_dve = sem("pt_dve"); pt_act = sem("pt_act"); pv_mm = sem("pv_mm"); summed = sem("summed")
        loop_dve = sem("loop_dve")
        var_ok = sem("var_ok"); rstd_ok = sem("rstd_ok")
        dchain = sem("dchain"); pchain = sem("pchain")
        normed = [sem(f"normed{i}") for i in range(5)]
        tr_mm = [sem(f"tr_mm{i}") for i in range(5)]
        tr_hi_ok = [sem(f"tr_hi_ok{i}") for i in range(5)]
        tr_lo_ok = [sem(f"tr_lo_ok{i}") for i in range(4)]
        q_mm = sem("q_mm"); q_out = sem("q_out")
        o_mm = sem("o_mm"); o_out = sem("o_out")
        q2_mm = sem("q2_mm"); k2_mm = sem("k2_mm"); v2_mm = sem("v2_mm")
        wide_ok = sem("wide_ok"); norm_hi_ok = sem("norm_hi_ok"); norm_lo_ok = sem("norm_lo_ok"); cleared = sem("cleared")
        q2_act = sem("q2_act"); q2_out = sem("q2_out"); k2_out = sem("k2_out"); v2_out = sem("v2_out")
        s2_mm = sem("s2_mm"); s2_clamped = sem("s2_clamped"); e2_ok = sem("e2_ok"); pv2_mm = sem("pv2_mm"); pv2_out = sem("pv2_out")
        o2_mm = sem("o2_mm"); o2_out = sem("o2_out")
        g_mm = sem("g_mm"); g_sub = sem("g_sub"); g_exp = sem("g_exp"); g_ok = sem("g_ok"); pt_g = sem("pt_g")
        slot_ok = sem("slot_ok"); slot_mm = sem("slot_mm"); onehot_ok = sem("onehot_ok"); weighted_ok = sem("weighted_ok")
        xin_mm = sem("xin_mm"); xin_dve = sem("xin_dve"); xin_act = sem("xin_act")
        back_mm = sem("back_mm"); back_ok = sem("back_ok")
        raw_in = [sem(f"raw_in{i}") for i in range(2 * NQ)]
        hi_ok = sem("hi_ok"); lo_ok = sem("lo_ok")
        tile_mm = sem("tile_mm")
        x_now_ok = sem("x_now_ok"); xin_hi_ok = sem("xin_hi_ok"); xin_staged = sem("xin_staged"); back_staged = sem("back_staged")
        gelu_ok = sem("gelu_ok"); ht_mm = sem("ht_mm"); ht_hi_ok = sem("ht_hi_ok"); ht_lo_ok = sem("ht_lo_ok")
        y_ok = sem("y_ok"); y_hi_ok = sem("y_hi_ok"); y_lo_ok = sem("y_lo_ok"); sc_mm = sem("sc_mm")
        rounded_ok = sem("rounded_ok"); res_ok = sem("res_ok"); stored = sem("stored")

        SPLITS = ((wq_s, 0, in_wq), (wo_s, 2, in_wo), (sq_s, 3, in_sq), (sv_s, 1, in_sv), (sk_s, 0, in_sk), (so_s, 3, in_so))
        TURN_BANKS = [[0, 1, 2, 3], [4, 5, 6, 7], [4, 5, 6, 7], [4] * 4, [4] * 4]
        V2_BANKS = [0, 1, 2, 4]

        def turned(i, b):
            return banks[TURN_BANKS[i][b]].rearrange("p (k t) -> p k t", k=KC)

        def of_batch(tensor, b):
            return tensor[:, :, b * T:(b + 1) * T]

        def chunk_j(eng, t):
            return eng.value_load(table[0:1, bass.ds(t, 1)], min_val=0, max_val=NJ - 1)

        def chunk_b(eng, t):
            return eng.value_load(table[0:1, bass.ds(t + (NJ + 1), 1)], min_val=0, max_val=B - 1)

        def last_chunk(eng):
            eng.wait_ge(table_ok, 2)
            return eng.value_load(table[0:1, 2 * (NJ + 1):2 * (NJ + 1) + 1], min_val=B - 1, max_val=NJ - 1)

        def w_tile(e, i):
            if i < NQ:
                w = w1[bass.ds(e, 1), :, i * D:(i + 1) * D]
            else:
                w = w2[bass.ds(e, 1), (i - NQ) * D:(i - NQ + 1) * D, :]
            return w.rearrange("a (k p) n -> p (a k) n", p=P)

        def prime(eng, *sems):
            for s in sems:
                eng.sem_inc(s, 1)

        block = ctx.enter_context(nc.Block())

        @block.sync
        def _(sp):
            sp.dma_start(mask_s[:], key_mask).then_inc(in_mask, 16)
            sp.dma_start(kb_s[:], key_bias).then_inc(in_mask, 16)
            sp.dma_start(x_s[:], x.rearrange("b t d -> t b d")).then_inc(in_x, 16)
            sp.dma_start(wk_s, wk.rearrange("(k p) n -> p k n", p=P)).then_inc(in_wk, 16)
            for i, v in enumerate((bq, bk, sbq, sbk)):
                sp.dma_start(cols[:, i, :], v).then_inc(in_cols, 16)
            sp.dma_start(bv_b[:], bv.partition_broadcast(P)).then_inc(in_cols, 16)
            sp.dma_start(wq_s, wq.rearrange("(k p) n -> p k n", p=P)).then_inc(in_wq, 16)

            def load_chunk(t):
                j = chunk_j(sp, t)
                sp.dma_start(ctx_s[:], ctx_t[bass.ds(j, 1)].rearrange("a p k n -> (a p) k n")).then_inc(ctx_in, 16)

            def load_bias(t):
                j = chunk_j(sp, t)
                sp.wait_ge(s_mm, t + 1)
                sp.dma_start(bias3[0:3, :], rows3[bass.ds(j, 1)].rearrange("a r n -> (a r) n")).then_inc(bias_in, 16)

            sp.wait_ge(rows_ok, 1)
            sp.dma_start(rows3, kb_3[:]).then_inc(rows_out, 16)
            last = last_chunk(sp)
            load_chunk(0)
            sp.dma_start(wv_s, wv.rearrange("(k p) n -> p k n", p=P)).then_inc(in_wv, 16)
            sp.wait_ge(rows_out, 16)
            sp.wait_ge(consts, 6)
            with sp.Fori(0, last) as t:
                load_bias(t)
                sp.wait_ge(v_mm, t + 2)
                load_chunk(t + 1)
            load_bias(last)
            sp.wait_ge(v_out, last + 1)
            sp.dma_start(bv_b[:], sbv.partition_broadcast(P)).then_inc(in_sb, 16)
            sp.dma_start(bo_b[:], sbo.partition_broadcast(P)).then_inc(in_sb, 16)
            sp.wait_ge(v_mm, last + 2)
            sp.wait_ge(att_lo_ok, 5)
            for i in range(2 * NQ):
                if i == 6:
                    sp.wait_ge(s2_mm, 2 * B)
                sp.dma_start(att_w[:, i], w_tile(0, i)).then_inc(raw_in[i], 16)
            sp.wait_ge(lo_ok, SLOTS)
            with sp.Fori(1, E) as e:
                for i in range(2 * NQ):
                    sp.wait_ge(lo_ok, e * 8 + (i - 7))
                    sp.dma_start(att_w[:, i], w_tile(e, i)).then_inc(raw_in[i], 16)
            for b in range(B):
                sp.wait_ge(res_ok, b + 1)
                sp.dma_start(out[b], x_s[:, b]).then_inc(stored, 16)
            sp.wait_ge(stored, 16 * B)

        @block.gpsimd
        def _(pool):
            g = nc.gpsimd
            def inverse_roots(n):
                for b in range(B):
                    pool.wait_ge(var_ok, n * B + b + 1)
                    g.tensor_tensor(rstd[:, b:b + 1], rstd[:, b:b + 1], minus_half[:, b:b + 1], ALU.pow).then_inc(rstd_ok, 1)

            g.memset(ident[:], 0.0).then_inc(pchain, 1)
            g.memset(minus_half[:], -0.5).then_inc(pchain, 1)
            g.memset(tri[:], 1.0).then_inc(pchain, 1)
            g.memset(ones3[:], 0.0).then_inc(pchain, 1)
            g.iota(idx[:, 0:1], pattern=[[0, 1]], base=0, channel_multiplier=1,
                   allow_small_or_imprecise_dtypes=True).then_inc(consts, 1)
            g.iota(slots[:], pattern=[[1, NJ + 1]], base=0, channel_multiplier=0,
                   allow_small_or_imprecise_dtypes=True).then_inc(consts, 1)
            g.iota(iota_s[:], pattern=[[1, CAP]], base=1, channel_multiplier=0,
                   allow_small_or_imprecise_dtypes=True).then_inc(consts, 1)
            pool.wait_ge(pchain, 4)
            g.affine_select(out=ident[:], in_=ident[:], compare_op=ALU.not_equal, fill=1.0, base=0,
                            pattern=[[-1, P]], channel_multiplier=1).then_inc(consts, 1)
            g.affine_select(out=tri[:], in_=tri[:], compare_op=ALU.is_gt, fill=0.0, base=0,
                            pattern=[[1, NJ]], channel_multiplier=-1).then_inc(consts, 1)
            g.memset(bias3[:], 0.0).then_inc(consts, 1)
            g.memset(ones3[0:3, :], 1.0).then_inc(consts, 1)
            g.memset(idx[:, 5:6], 1.0).then_inc(consts, 1)
            g.memset(v_s[:, :, :, DH:HV], 1.0).then_inc(consts, 1)
            g.memset(state[:], 0.0).then_inc(consts, 1)
            g.memset(run_max[:], -MASKED).then_inc(consts, 1)
            inverse_roots(0)
            last = last_chunk(pool)
            pool.wait_ge(q_out, 4)
            with pool.Fori(0, last + 1) as t:
                b = chunk_b(pool, t)
                pool.wait_ge(s_mm, t + 1)
                g.tensor_copy(q_now[:], qt[:, bass.ds(b, 1)].rearrange("p a k n -> p (a k) n")).then_inc(q_staged, 1)
            inverse_roots(1)
            for i in range(2):
                pool.wait_ge(att_lo_ok, 5 + i)
                g.memset(att_w[:, 6 + i], 0.0).then_inc(cleared, 1)
            inverse_roots(2)
            pool.wait_ge(o2_mm, B)
            for b in range(B):
                pool.wait_ge(norm_hi_ok, b + 1)
                if b:
                    pool.wait_ge(norm_lo_ok, b)
                g.tensor_tensor(norm_lo[:, b], norm[:, b], norm_hi[:, b], ALU.subtract).then_inc(norm_lo_ok, 1)
            pool.wait_ge(norm_lo_ok, B)
            pool.wait_ge(raw_in[3], 16)
            pool.wait_ge(lo_ok, 3)
            g.tensor_copy(w_hi[:, 3], att_w[:, 3]).then_inc(hi_ok, 1)
            pool.wait_ge(hi_ok, 4)
            g.tensor_tensor(w_lo[:, 3], att_w[:, 3], w_hi[:, 3], ALU.subtract).then_inc(lo_ok, 1)
            pool.wait_ge(lo_ok, 4)

            def stage_input(e):
                pool.wait_ge(tile_mm, e * 8 - 4)
                now = xin[:, :, bass.ds(e, 1)].rearrange("p k a n -> p (k a) n")
                g.tensor_copy(x_now[:], now).then_inc(x_now_ok, 1)
                g.tensor_copy(xin_hi[:], now).then_inc(x_now_ok, 1)
                pool.wait_ge(x_now_ok, e * 2)
                g.tensor_tensor(xin_lo[:], x_now[:], xin_hi[:], ALU.subtract).then_inc(xin_staged, 1)

            def stage_back(e):
                g.tensor_copy(back_now[:], back[:, bass.ds(e, 1), :].rearrange("p a n -> p (a n)")).then_inc(back_staged, 1)

            pool.wait_ge(back_ok, 4)
            stage_back(0)
            with pool.Fori(1, E) as e:
                stage_input(e)
                pool.wait_ge(sc_mm, e)
                stage_back(e)

        @block.scalar
        def _(act):
            a = nc.scalar
            prime(act, pt_act)
            def split_att(n):
                w, slot, landed = SPLITS[n]
                act.wait_ge(landed, 16)
                a.copy(w_hi[:, slot], w).then_inc(att_hi_ok, 1)

            def transposed(i, b):
                act.wait_ge(tr_mm[i], b + 1)
                a.copy(of_batch(tr_hi, b), turned(i, b)).then_inc(tr_hi_ok[i], 1)

            def k_evacuate(t):
                act.wait_ge(k_mm, t + 1)
                for c in range(KC):
                    ins = a.activation(kt_s[:, c], pk[:, c * P:(c + 1) * P], ACT.Identity, bias=cols[:, 1, c:c + 1])
                ins.then_inc(k_out, 1)

            def softmax_chunk(t, more):
                act.wait_ge(negm_ok, 2 * t + 2)
                act.wait_ge(summed, t + 1)
                a.activation(alpha[:], mdiff[:], ACT.Exp).then_inc(alpha_ok, 1)
                for c in range(STRIPS):
                    for g in range(KC):
                        h = c * KC + g
                        ins = a.activation(big_a[:, h], ps[:, c, g * P:(g + 1) * P], ACT.Exp, bias=negm[:, h:h + 1])
                    ins.then_inc(p_ok, 1)
                if more:
                    k_evacuate(t + 1)
                act.wait_ge(pt_mm, 4 * t + 4)
                a.copy(big_b[:, 3 * KC:4 * KC].rearrange("p h k -> p (h k)"), ps[:, 3]).then_inc(pt_act, 1)

            last = last_chunk(act)
            split_att(0)
            act.dma_start(wo_s, wo.rearrange("(k p) n -> p k n", p=P)).then_inc(in_wo, 16)
            act.dma_start(bo_b[:], bo.partition_broadcast(P)).then_inc(in_bo, 16)
            for w, s, landed in ((sq, sq_s, in_sq), (sv, sv_s, in_sv), (sk, sk_s, in_sk), (so, so_s, in_so)):
                act.dma_start(s, w.rearrange("(k p) n -> p k n", p=P)).then_inc(landed, 16)
            act.dma_start(gate_s[:], gate.rearrange("(k p) e -> p k e", p=P)).then_inc(in_gate, 16)
            for b in range(B):
                transposed(0, b)
            split_att(1)
            act.wait_ge(in_cols, 80)
            k_evacuate(0)
            split_att(2)
            split_att(3)
            act.wait_ge(q_mm, KC)
            split_att(4)
            with act.Fori(0, last) as t:
                softmax_chunk(t, True)
            softmax_chunk(last, False)
            for i in (1, 2):
                for b in range(B):
                    transposed(i, b)
            for c in range(KC):
                act.wait_ge(q2_mm, c + 1)
                a.activation(qt[:, :, c], banks[4 + c].rearrange("p (b t) -> p b t", b=B), ACT.Identity,
                             bias=cols[:, 2, c:c + 1]).then_inc(q2_act, 1)
            split_att(5)

            def split_first(i, used):
                act.wait_ge(raw_in[i], 16)
                act.wait_ge(used, KC)
                a.copy(w_hi[:, i], att_w[:, i]).then_inc(hi_ok, 1)

            def widen(b):
                act.wait_ge(q2_out, KC)
                act.wait_ge(cleared, min(b, 1) + 1)
                if b >= 2:
                    act.wait_ge(s2_mm, 2 * b - 2)
                for c in range(STRIPS):
                    r = slice(c * DH, (c + 1) * DH)
                    a.copy(q_wide[r, b % 2, c], qt[r, b]).then_inc(wide_ok, 1)

            for c in range(KC):
                act.wait_ge(k2_mm, c + 1)
                a.activation(kt2[:, :, c], ps[:, c].rearrange("p (b t) -> p b t", b=B), ACT.Identity,
                             bias=cols[:, 3, c:c + 1]).then_inc(q2_act, 1)
                if c == 1:
                    split_first(2, o_mm)
                else:
                    if c < 3:
                        widen(c // 2)
            split_first(0, k2_mm)

            def exps2(u):
                half = big_a if u % 2 == 0 else big_b
                act.wait_ge(s2_clamped, u + 1)
                if u >= 2:
                    act.wait_ge(pv2_mm, u - 1)
                a.activation(half[:, 8:16], half[:, 0:8], ACT.Exp).then_inc(e2_ok, 1)

            def gate_transposed(b):
                act.wait_ge(tr_mm[4], b + 1)
                a.copy(tr_gate[:, b], turned(4, b)).then_inc(tr_hi_ok[4], 1)

            exps2(0)
            exps2(1)
            widen(2)
            split_first(1, v2_mm)
            for u in range(2 * B):
                if u + 2 < 2 * B:
                    exps2(u + 2)
                if u == 1:
                    widen(3)
                if u == 2:
                    transposed(3, 0)
                if u == 3:
                    transposed(3, 1)
                if u == 5:
                    gate_transposed(0)
                    transposed(3, 2)
                if u == 6:
                    gate_transposed(1)
            transposed(3, B - 1)
            gate_transposed(2)
            for b in range(B):
                if b == B - 1:
                    gate_transposed(3)
                act.wait_ge(normed[4], b + 1)
                a.copy(norm_hi[:, b], norm[:, b]).then_inc(norm_hi_ok, 1)
            act.wait_ge(g_sub, 1)
            a.activation(gsm[:, 2], gsm[:, 1], ACT.Exp).then_inc(g_exp, 1)
            for i in range(4):
                c = 2 * i + 1
                act.wait_ge(xin_mm, c + 1)
                a.copy(xin[:, c % 4].rearrange("p e (b s) -> p b e s", b=B)[:, 2 * (c // 4):2 * (c // 4) + 2],
                       banks[c].rearrange("p (b e s) -> p b e s", b=2, e=E)).then_inc(xin_act, 1)
            act.wait_ge(xin_dve, 4)
            act.wait_ge(xin_act, 4)
            a.copy(xin_hi[:], xin[:, :, 0]).then_inc(xin_hi_ok, 1)

            def split_hi(e, i):
                act.wait_ge(raw_in[i], e * 16 + 16)
                act.wait_ge(tile_mm, e * 8 + (i - SLOTS + 1))
                a.copy(w_hi[:, i % SLOTS], att_w[:, i]).then_inc(hi_ok, 1)

            def gelu(e, q):
                act.wait_ge(tile_mm, e * 8 + (q + 1))
                if q >= 2 or not isinstance(e, int):
                    act.wait_ge(ht_mm, e * 4 + (q - 1))
                a.activation(h_s[:, q % 2], (pk, pv)[q % 2][:], ACT.Gelu_apprx_tanh).then_inc(gelu_ok, 1)

            def transposed_hi(e, q):
                act.wait_ge(ht_mm, e * 4 + (q + 1))
                a.copy(ht_hi[:, q * 4:q * 4 + 4].rearrange("p c n -> p (c n)"), po[:, 1]).then_inc(ht_hi_ok, 1)

            def expert(e, more):
                gelu(e, 0)
                split_hi(e, 4)
                gelu(e, 1)
                transposed_hi(e, 0)
                split_hi(e, 5)
                gelu(e, 2)
                transposed_hi(e, 1)
                split_hi(e, 6)
                gelu(e, 3)
                transposed_hi(e, 2)
                split_hi(e, 7)
                transposed_hi(e, 3)
                if more:
                    for i in range(SLOTS):
                        split_hi(e + 1, i)
                act.wait_ge(y_ok, e + 1)
                if not isinstance(e, int) or e > 0:
                    act.wait_ge(sc_mm, e)
                a.copy(y_hi[:], y_s[:]).then_inc(y_hi_ok, 1)

            expert(0, True)
            with act.Fori(1, E - 1) as e:
                expert(e, True)
            expert(E - 1, False)

        @block.vector
        def _(dve):
            v = nc.vector
            links = [0]
            ln_count = [0]

            def link(ins):
                ins.then_inc(dchain, 1)
                links[0] += 1
                dve.wait_ge(dchain, links[0])

            def statistics(b):
                link(v.bn_stats(stats[:, b], x_s[:, b]))
                link(v.bn_aggr(aggr[:, b], stats[:, b]))
                v.tensor_scalar(rstd[:, b:b + 1], aggr[:, b, 1:2], EPS_LN, None, ALU.add).then_inc(var_ok, 1)

            def normed_batch(i, b):
                ln_count[0] += 1
                dve.wait_ge(rstd_ok, ln_count[0])
                v.tensor_scalar(norm[:, b], x_s[:, b], aggr[:, b, 0:1], rstd[:, b:b + 1],
                                ALU.subtract, ALU.mult).then_inc(normed[i], 1)

            def transposed(i, b):
                dve.wait_ge(tr_hi_ok[i], b + 1)
                v.tensor_tensor(of_batch(tr_lo, b), turned(i, b), of_batch(tr_hi, b), ALU.subtract).then_inc(tr_lo_ok[i], 1)

            def split_att(n):
                w, slot, _ = SPLITS[n]
                dve.wait_ge(att_hi_ok, n + 1)
                v.tensor_tensor(w_lo[:, slot], w, w_hi[:, slot], ALU.subtract).then_inc(att_lo_ok, 1)

            def heads(ap):
                return ap.rearrange("p (g j d) -> p j g d", j=STRIPS, d=DH)

            prime(dve, summed, pt_dve)
            dve.wait_ge(in_mask, 32)
            dve.wait_ge(consts, 11)
            v.tensor_reduce(idx[:, 3:4], mask_s[:], AX.X, ALU.max)
            link(v.tensor_scalar(idx[:, 2:3], idx[:, 0:1], float(NCH), None, ALU.is_ge))
            for b in range(2, B):
                link(v.scalar_tensor_tensor(idx[:, 2:3], idx[:, 0:1], float(b * NCH), idx[:, 2:3], ALU.is_ge, ALU.add))
            link(v.scalar_tensor_tensor(idx[:, 1:2], idx[:, 2:3], -float(NCH), idx[:, 0:1], ALU.mult, ALU.add))
            link(v.tensor_scalar(idx[:, 6:7], idx[:, 1:2], float(NCH - 1), None, ALU.is_equal))
            v.tensor_tensor(idx[:, 7:8], idx[:, 3:4], idx[:, 6:7], ALU.max).then_inc(act_ok, 1)
            link(v.tensor_scalar(kb_m[:], mask_s[:], 1.0, MASKED, ALU.subtract, ALU.mult))
            link(v.tensor_tensor(kb_m[:], kb_m[:], kb_s[:], ALU.add))
            link(v.tensor_copy(kb_3[:, 0], kb_m[:]))
            link(v.tensor_tensor(kb_m[:], kb_m[:], kb_3[:, 0], ALU.subtract))
            link(v.tensor_copy(kb_3[:, 1], kb_m[:]))
            link(v.tensor_tensor(kb_m[:], kb_m[:], kb_3[:, 1], ALU.subtract))
            v.tensor_copy(kb_3[:, 2], kb_m[:]).then_inc(rows_ok, 1)
            dve.wait_ge(place_mm, 1)
            link(v.tensor_copy(idx[:, 4:5], pv[0:NJ, 0:1]))
            v.tensor_scalar(pick[:], slots[:], idx[:, 4:5], idx[:, 7:8], ALU.is_equal, ALU.mult).then_inc(pick_ok, 1)
            dve.wait_ge(table_mm, 1)
            n_at = 2 * (NJ + 1)
            v.tensor_copy(table[:, 0:n_at], pv[0:1, 0:n_at]).then_inc(table_ok, 1)
            v.tensor_scalar(table[:, n_at:n_at + 1], pv[0:1, n_at:n_at + 1], -1.0, None, ALU.add).then_inc(table_ok, 1)

            dve.wait_ge(in_x, 16)
            for b in range(B):
                statistics(b)
            for b in range(B):
                normed_batch(0, b)
            split_att(0)
            for b in range(B):
                transposed(0, b)
            def v_evacuate(t):
                dve.wait_ge(v_mm, t + 2)
                v.tensor_tensor(v_s[:, 0].rearrange("p (j g) d -> p j g d", j=STRIPS)[:, :, :, 0:DH],
                                heads(pv[:]), heads(bv_b[:]), ALU.add).then_inc(v_out, 1)

            dve.wait_ge(in_bo, 16)
            for b in range(B):
                ins = v.tensor_tensor(x_s[:, b], x_s[:, b], bo_b[:], ALU.add)
            link(ins)
            split_att(1)
            dve.wait_ge(in_cols, 80)
            for c in range(KC):
                if c == 2:
                    split_att(2)
                dve.wait_ge(q_mm, c + 1)
                v.tensor_scalar(qt[:, :, c], ps[:, c].rearrange("p (b t) -> p b t", b=B), cols[:, 0, c:c + 1],
                                SCALE, ALU.add, ALU.mult).then_inc(q_out, 1)
            split_att(3)
            v_evacuate(0)
            split_att(4)
            last = last_chunk(dve)

            def softmax_chunk(t, more):
                b = chunk_b(dve, t)
                rm = run_max[:, bass.ds(b, 1)].rearrange("p a h -> p (a h)")
                st = state[:, bass.ds(b, 1)].rearrange("p a h d -> p (a h) d")
                dve.wait_ge(s_mm, t + 2)
                v.tensor_reduce(mc[:], ps[:].rearrange("p c (g k) -> p (c g) k", k=P), AX.X, ALU.max).then_inc(loop_dve, 1)
                dve.wait_ge(loop_dve, 4 * t + 1)
                v.tensor_tensor(mnew[:], mc[:], rm, ALU.max).then_inc(loop_dve, 1)
                dve.wait_ge(loop_dve, 4 * t + 2)
                v.tensor_scalar(negm[:], mnew[:], -1.0, None, ALU.mult).then_inc(negm_ok, 1)
                v.tensor_tensor(mdiff[:], rm, mnew[:], ALU.subtract).then_inc(negm_ok, 1)
                dve.wait_ge(negm_ok, 2 * t + 2)
                v.tensor_tensor(rm, mc[:], rm, ALU.max).then_inc(loop_dve, 1)
                dve.wait_ge(alpha_ok, t + 1)
                v.tensor_tensor(st, st, alpha[:].unsqueeze(2).broadcast_to([P, H, HV]), ALU.mult).then_inc(loop_dve, 1)
                for c in range(3):
                    dve.wait_ge(pt_mm, 4 * t + c + 1)
                    v.tensor_copy(big_b[:, c * KC:(c + 1) * KC].rearrange("p h k -> p (h k)"), ps[:, c]).then_inc(pt_dve, 1)
                dve.wait_ge(pv_mm, t + 1)
                dve.wait_ge(loop_dve, 4 * t + 4)
                for c in range(2):
                    half = st[:, 8 * c:8 * c + 8]
                    ins = v.tensor_tensor(half, half, po[:, c, 0:8 * HV].rearrange("p (h d) -> p h d", d=HV), ALU.add)
                ins.then_inc(summed, 1)
                if more:
                    v_evacuate(t + 1)

            with dve.Fori(0, last) as t:
                softmax_chunk(t, True)
            softmax_chunk(last, False)

            dve.wait_ge(summed, last + 2)
            link(v.tensor_scalar(norm_c[:], run_max[:], -0.1 * MASKED, None, ALU.is_gt))
            link(v.tensor_tensor(run_max[:], norm_c[:], state[:, :, :, DH], ALU.mult))
            link(v.reciprocal(run_max[:], run_max[:]))
            link(v.tensor_tensor(norm_c[:], norm_c[:], run_max[:], ALU.mult))
            for b in range(B):
                v.tensor_tensor(heads(norm[:, b]), state[:, b].rearrange("p (j g) d -> p j g d", j=STRIPS)[:, :, :, 0:DH],
                                norm_c[:, b].rearrange("p (j g) -> p j g", j=STRIPS).unsqueeze(3).broadcast_to([P, STRIPS, KC, DH]),
                                ALU.mult).then_inc(normed[1], 1)
            for b in range(B):
                transposed(1, b)

            def cross_output(b):
                dve.wait_ge(o_mm, b + 1)
                link(v.tensor_tensor(x_s[:, b], x_s[:, b], ps[:, b], ALU.add))
                statistics(b)

            for b in range(B):
                cross_output(b)
                if b:
                    normed_batch(2, b - 1)
                if b == B - 2:
                    transposed(2, 0)
            transposed(2, 1)
            normed_batch(2, B - 1)
            transposed(2, 2)

            def values_out(b):
                dst = v_s[:, b].rearrange("p (j g) d -> p j g d", j=STRIPS)[:, :, :, 0:DH]
                dve.wait_ge(v2_mm, b + 1)
                link(v.tensor_tensor(dst, heads(banks[V2_BANKS[b]]), heads(bv_b[:]), ALU.add))
                v.tensor_scalar(dst, dst, LO, HI, ALU.max, ALU.min).then_inc(v2_out, 1)

            dve.wait_ge(in_sb, 32)
            values_out(0)
            values_out(1)
            transposed(2, 3)
            values_out(2)
            for c in range(KC):
                dve.wait_ge(q2_act, c + 1)
                link(v.tensor_scalar(qt[:, :, c], qt[:, :, c], SCALE, LO, ALU.mult, ALU.max))
                v.tensor_scalar(qt[:, :, c], qt[:, :, c], HI, None, ALU.min).then_inc(q2_out, 1)
            def split_first(n, i):
                dve.wait_ge(hi_ok, n + 1)
                v.tensor_tensor(w_lo[:, i], att_w[:, i], w_hi[:, i], ALU.subtract).then_inc(lo_ok, 1)

            split_att(5)
            for c in range(KC):
                dve.wait_ge(q2_act, KC + c + 1)
                v.tensor_scalar(kt2[:, :, c], kt2[:, :, c], LO, HI, ALU.max, ALU.min).then_inc(k2_out, 1)
                if c == 1:
                    split_first(0, 2)
            values_out(B - 1)

            def clamp_scores(u):
                half = big_a if u % 2 == 0 else big_b
                dve.wait_ge(s2_mm, u + 1)
                if u >= 2:
                    dve.wait_ge(e2_ok, u - 1)
                v.tensor_scalar(half[:, 0:8].rearrange("p h k -> p (h k)"),
                                ps[:, 2 * (u % 2):2 * (u % 2) + 2].rearrange("p c n -> p (c n)"),
                                LO, HI, ALU.max, ALU.min).then_inc(s2_clamped, 1)

            def normalise(u):
                b, c = u // 2, u % 2
                o3 = po[:, c, 0:8 * HV].rearrange("p (h d) -> p h d", d=HV)
                dve.wait_ge(pv2_mm, u + 1)
                if u:
                    dve.wait_ge(pv2_out, u)
                link(v.reciprocal(mc[:, 0:8], o3[:, :, DH]))
                dst = heads(norm[:, b])[:, 2 * c:2 * c + 2]
                ins = v.tensor_tensor(dst, o3[:, :, 0:DH].rearrange("p (j g) d -> p j g d", j=2),
                                      mc[:, 0:8].rearrange("p (j g) -> p j g", j=2).unsqueeze(3).broadcast_to([P, 2, KC, DH]),
                                      ALU.mult)
                ins.then_inc(pv2_out, 1)
                if c == 1:
                    dve.wait_ge(pv2_out, u + 1)
                    v.tensor_scalar(norm[:, b], norm[:, b], LO, HI, ALU.max, ALU.min).then_inc(normed[3], 1)

            def self_bias(b):
                dve.wait_ge(o2_mm, b + 1)
                link(v.tensor_tensor(norm[:, b], pv[:], bo_b[:], ALU.add))
                v.tensor_scalar(norm[:, b], norm[:, b], LO, HI, ALU.max, ALU.min).then_inc(o2_out, 1)

            def self_residual(b):
                dve.wait_ge(o2_out, b + 1)
                link(v.tensor_tensor(x_s[:, b], x_s[:, b], norm[:, b], ALU.add))
                statistics(b)

            clamp_scores(0)
            clamp_scores(1)
            split_first(1, 0)
            for u in range(2 * B):
                normalise(u)
                if u == 7:
                    self_residual(2)
                if u + 2 < 2 * B:
                    clamp_scores(u + 2)
                if u == 2:
                    transposed(3, 0)
                if u in (3, 5):
                    b = u // 2 - 1
                    self_bias(b)
                    transposed(3, b + 1)
                    self_residual(b)
                    normed_batch(4, b)
                if u == 6:
                    self_bias(2)
                if u == 0:
                    split_first(2, 1)
            transposed(3, 3)
            normed_batch(4, 2)
            self_bias(3)
            self_residual(3)
            normed_batch(4, 3)
            def by_batch(i):
                return gsm[:, i].rearrange("p (b e) -> p b e", b=B)

            def wide(i):
                return gred[:, i].unsqueeze(2).broadcast_to([P, B, E])

            g_psum = logits[:].rearrange("p (b e) -> p b e", b=B)
            dve.wait_ge(g_mm, B)
            link(v.tensor_reduce(gred[:, 0], g_psum, AX.X, ALU.max))
            v.tensor_tensor(by_batch(1), g_psum, wide(0), ALU.subtract).then_inc(g_sub, 1)
            dve.wait_ge(g_exp, 1)
            link(v.tensor_reduce(gred[:, 1], by_batch(2), AX.X, ALU.add))
            link(v.reciprocal(gred[:, 2], gred[:, 1]))
            v.tensor_tensor(by_batch(3), by_batch(2), wide(2), ALU.mult).then_inc(g_ok, 1)
            dve.wait_ge(pt_g, 1)
            link(v.tensor_copy(prob_t, pv[0:B * E, 0:T]))
            src = prob_t
            for r in range(CAP // 8):
                link(v.max(top8[:], src))
                link(v.match_replace(work[:, r % 2], top8[:], src, -1.0))
                src = work[:, r % 2]
            link(v.tensor_scalar(chosen[:, 0], src, 0.0, None, ALU.is_lt))
            link(v.memset(chosen[:, 2], 0.0))
            link(v.tensor_tensor_scan(chosen[:, 1], chosen[:, 0], chosen[:, 2], 0.0, ALU.add, ALU.add))
            v.tensor_tensor(chosen[:, 2], chosen[:, 0], chosen[:, 1], ALU.mult).then_inc(slot_ok, 1)
            dve.wait_ge(slot_mm, 1)
            link(v.tensor_copy(slot_t[:], pk[:, 0:B * E]))
            be = "p b e s -> p (b e) s"
            v.tensor_tensor(onehot.rearrange(be), slot_t[:].unsqueeze(2).broadcast_to([P, B * E, CAP]),
                            iota_s[:].unsqueeze(1).broadcast_to([P, B * E, CAP]), ALU.is_equal).then_inc(onehot_ok, 1)
            dve.wait_ge(onehot_ok, 1)
            v.tensor_tensor(weighted.rearrange("p e b s -> p b e s"), onehot,
                            by_batch(3).unsqueeze(3).broadcast_to([P, B, E, CAP]), ALU.mult).then_inc(weighted_ok, 1)
            for i in range(4):
                c = 2 * i
                dve.wait_ge(xin_mm, c + 1)
                v.tensor_copy(xin[:, c % 4].rearrange("p e (b s) -> p b e s", b=B)[:, 2 * (c // 4):2 * (c // 4) + 2],
                              banks[c].rearrange("p (b e s) -> p b e s", b=2, e=E)).then_inc(xin_dve, 1)
            dve.wait_ge(xin_hi_ok, 1)
            v.tensor_tensor(xin_lo[:], xin[:, :, 0], xin_hi[:], ALU.subtract).then_inc(xin_staged, 1)
            for i in range(2):
                dve.wait_ge(back_mm, i + 1)
                v.tensor_reduce(gcol[:, 4 * i:4 * i + 4], (pk, pv)[i][:].rearrange("p (e t) -> p e t", e=4), AX.X, ALU.add).then_inc(back_ok, 1)
                v.tensor_scalar(back[:, 4 * i:4 * i + 4].rearrange("p e t -> p (e t)"), (pk, pv)[i][:], 0.0, None, ALU.is_gt).then_inc(back_ok, 1)
            def split_lo(e, i):
                dve.wait_ge(hi_ok, e * 8 + (i + 1))
                v.tensor_tensor(w_lo[:, i % SLOTS], att_w[:, i], w_hi[:, i % SLOTS], ALU.subtract).then_inc(lo_ok, 1)

            def transposed_lo(e, q):
                dve.wait_ge(ht_hi_ok, e * 4 + (q + 1))
                part = slice(q * 4, q * 4 + 4)
                v.tensor_tensor(ht_lo[:, part].rearrange("p c n -> p (c n)"), po[:, 1],
                                ht_hi[:, part].rearrange("p c n -> p (c n)"), ALU.subtract).then_inc(ht_lo_ok, 1)

            def expert(e, more):
                for q in range(NQ):
                    split_lo(e, NQ + q)
                    transposed_lo(e, q)
                if more:
                    for i in range(SLOTS - 1):
                        split_lo(e + 1, i)
                dve.wait_ge(tile_mm, e * 8 + 8)
                if isinstance(e, int) and e == 0:
                    dve.wait_ge(back_ok, 4)
                else:
                    dve.wait_ge(y_lo_ok, e)
                v.tensor_tensor(y_s[:], po[:, 0], gcol[:, bass.ds(e, 1)].broadcast_to([P, D]), ALU.mult).then_inc(y_ok, 1)
                if more:
                    split_lo(e + 1, SLOTS - 1)
                dve.wait_ge(y_hi_ok, e + 1)
                v.tensor_tensor(y_lo[:], y_s[:], y_hi[:], ALU.subtract).then_inc(y_lo_ok, 1)

            expert(0, True)
            with dve.Fori(1, E - 1) as e:
                expert(e, True)
            expert(E - 1, False)
            dve.wait_ge(sc_mm, E)
            for b in range(B):
                v.tensor_copy(rounded[:, b], ps[:, b]).then_inc(rounded_ok, 1)
                dve.wait_ge(rounded_ok, b + 1)
                v.tensor_tensor(x_s[:, b], x_s[:, b], rounded[:, b], ALU.add).then_inc(res_ok, 1)

        @block.tensor
        def _(pe):
            mm = nc.tensor.matmul

            def k_project(t):
                pe.wait_ge(ctx_in, t * 16 + 16)
                if not isinstance(t, int):
                    pe.wait_ge(k_out, t)
                for g in range(KC):
                    for k in range(KC):
                        ins = mm(pk[:, g * P:(g + 1) * P], wk_s[:, k, g * P:(g + 1) * P], ctx_s[:, k], start=k == 0, stop=k == KC - 1)
                ins.then_inc(k_mm, 1)

            def v_project(t, k):
                if k == 0 and not isinstance(t, int):
                    pe.wait_ge(v_out, t)
                ins = mm(pv[:], ctx_s[:, k], wv_s[:, k], start=k == 0, stop=k == KC - 1, skip_group_check=True)
                if k == KC - 1:
                    ins.then_inc(v_mm, 1)

            def turn_batch(i, b):
                pe.wait_ge(normed[i], b + 1)
                for k in range(KC):
                    ins = nc.tensor.transpose(turned(i, b)[:, k], norm[:, b, k * P:(k + 1) * P], ident[:])
                ins.then_inc(tr_mm[i], 1)

            def product(dst, pairs):
                for n, (l, r) in enumerate(pairs):
                    ins = mm(dst, l, r, start=n == 0, stop=n == len(pairs) - 1, skip_group_check=True)
                return ins

            def project_t(slot, dst, done):
                for g in range(KC):
                    cols_g = slice(g * P, (g + 1) * P)
                    product(dst[g], [(w[:, slot, k, cols_g], t[:, k]) for k in range(KC)
                                     for w, t in ((w_hi, tr_hi), (w_lo, tr_hi), (w_hi, tr_lo))]).then_inc(done, 1)

            def project(slot, b, dst, done):
                now = slice(b * T, (b + 1) * T)
                product(dst, [(t[:, k, now], w[:, slot, k]) for k in range(KC)
                              for w, t in ((w_hi, tr_hi), (w_lo, tr_hi), (w_hi, tr_lo))]).then_inc(done, 1)

            prime(pe, v_mm, s_mm)
            pe.wait_ge(consts, 11)
            pe.wait_ge(act_ok, 1)
            mm(pv[0:NJ, 0:1], tri[:], idx[:, 7:8], start=True, stop=True).then_inc(place_mm, 1)
            pe.wait_ge(pick_ok, 1)
            mm(pv[0:1, 0:NJ + 1], idx[:, 0:1], pick[:], start=True, stop=True)
            mm(pv[0:1, NJ + 1:2 * (NJ + 1)], idx[:, 2:3], pick[:], start=True, stop=True)
            mm(pv[0:1, 2 * (NJ + 1):2 * (NJ + 1) + 1], idx[:, 7:8], idx[:, 5:6], start=True, stop=True).then_inc(table_mm, 1)
            last = last_chunk(pe)
            def scores(t):
                pe.wait_ge(bias_in, t * 16 + 16)
                pe.wait_ge(q_staged, t + 1)
                pe.wait_ge(k_out, t + 1)
                pe.wait_ge(pt_dve, t * 3 + 1)
                pe.wait_ge(pt_act, t + 1)
                for c in range(STRIPS):
                    mm(ps[:, c].rearrange("p (g k) -> p g k", g=KC), ones3[:], bias3[:].unsqueeze(1).broadcast_to([P, KC, P]),
                       start=True, stop=False, skip_group_check=True)
                for g in range(KC):
                    for c in range(STRIPS):
                        r = slice(c * DH, (c + 1) * DH)
                        ins = mm(ps[:, c, g * P:(g + 1) * P], q_now[r, g], kt_s[r, g], start=False, stop=True, skip_group_check=True)
                ins.then_inc(s_mm, 1)

            def turn_probs(t, c):
                pe.wait_ge(p_ok, t * 4 + (c + 1))
                for g in range(KC):
                    ins = nc.tensor.transpose(ps[:, c, g * P:(g + 1) * P], big_a[:, c * KC + g], ident[:])
                ins.then_inc(pt_mm, 1)

            def values(t, c):
                if c == 0:
                    pe.wait_ge(v_out, t + 1)
                    pe.wait_ge(summed, t + 1)
                if c < 3:
                    pe.wait_ge(pt_dve, t * 3 + (c + 2))
                else:
                    pe.wait_ge(pt_act, t + 2)
                for h in range(c * KC, (c + 1) * KC):
                    ins = mm(po[:, h // 8, (h % 8) * HV:(h % 8 + 1) * HV], big_b[:, h], v_s[:, 0, h], start=True, stop=True)
                if c == 3:
                    ins.then_inc(pv_mm, 1)

            def chunk(t, more):
                scores(t)
                if more:
                    k_project(t + 1)
                for c in range(STRIPS):
                    if more:
                        v_project(t + 1, c)
                    turn_probs(t, c)
                    if c:
                        values(t, c - 1)
                values(t, STRIPS - 1)

            pe.wait_ge(in_wk, 16)
            for b in range(B):
                turn_batch(0, b)
            k_project(0)
            pe.wait_ge(tr_lo_ok[0], B)
            pe.wait_ge(att_lo_ok, 1)
            project_t(0, banks[0:4], q_mm)
            pe.wait_ge(in_wv, 16)
            for k in range(KC):
                v_project(0, k)
            pe.wait_ge(q_out, 4)
            with pe.Fori(0, last) as t:
                chunk(t, True)
            chunk(last, False)

            for b in range(B):
                turn_batch(1, b)
            def cross_project(b):
                pe.wait_ge(tr_lo_ok[1], b + 1)
                project(2, b, banks[b], o_mm)

            def values_project(b):
                pe.wait_ge(tr_lo_ok[2], b + 1)
                project(1, b, banks[V2_BANKS[b]], v2_mm)

            pe.wait_ge(tr_lo_ok[1], B)
            cross_project(0)
            cross_project(1)
            cross_project(2)
            turn_batch(2, 0)
            cross_project(3)
            pe.wait_ge(att_lo_ok, 5)
            turn_batch(2, 1)
            values_project(0)
            turn_batch(2, 2)
            values_project(1)
            turn_batch(2, 3)
            values_project(2)
            pe.wait_ge(tr_lo_ok[2], B)
            project_t(3, banks[4:8], q2_mm)
            pe.wait_ge(v2_out, B - 1)
            project_t(0, banks[0:4], k2_mm)
            pe.wait_ge(q2_act, 1)
            values_project(3)

            def waits_scores2(u):
                pe.wait_ge(wide_ok, 4 * (u // 2 + 1))
                if u == 0:
                    pe.wait_ge(q2_out, KC)
                    pe.wait_ge(k2_out, KC)
                if u >= 2:
                    pe.wait_ge(s2_clamped, u - 1)

            def waits_values2(u):
                pe.wait_ge(e2_ok, u + 1)
                if u == 0:
                    pe.wait_ge(v2_out, B)
                if u >= 2:
                    pe.wait_ge(pv2_out, u - 1)

            def score2(u, n):
                b, g, c = u // 2, n // 2, 2 * (u % 2) + n % 2
                return mm(ps[:, c, g * P:(g + 1) * P], kt2[:, b, g], q_wide[:, b % 2, c, g], start=True, stop=True)

            def value2(u, n):
                b, c = u // 2, u % 2
                half = big_a if c == 0 else big_b
                return mm(po[:, c, n * HV:(n + 1) * HV], half[:, 8 + n], v_s[:, b, 8 * c + n], start=True, stop=True)

            def unit(u):
                waits_values2(u)
                more = u + 2 < 2 * B
                if more:
                    waits_scores2(u + 2)
                for n in range(8):
                    if more:
                        ins = score2(u + 2, n)
                        if n == 7:
                            ins.then_inc(s2_mm, 1)
                    ins = value2(u, n)
                ins.then_inc(pv2_mm, 1)

            def out_project(b):
                pe.wait_ge(tr_lo_ok[3], b + 1)
                pe.wait_ge(att_lo_ok, 6)
                if b:
                    pe.wait_ge(o2_out, b)
                project(3, b, pv[:], o2_mm)

            def turn_out(b):
                if b == 1:
                    pe.wait_ge(tr_lo_ok[3], 1)
                if b >= 2:
                    pe.wait_ge(tr_hi_ok[4], b - 1)
                turn_batch(3, b)

            def turn_gate(b):
                pe.wait_ge(tr_lo_ok[3], min(b + 2, B))
                if b == B - 1:
                    pe.wait_ge(tr_hi_ok[4], b)
                turn_batch(4, b)

            def gate_project(b, u):
                pe.wait_ge(tr_hi_ok[4], b + 1)
                pe.wait_ge(pv2_out, u)
                for k in range(KC):
                    ins = mm(logits[:, b * E:(b + 1) * E], tr_gate[:, b, k], gate_s[:, k], start=k == 0, stop=k == KC - 1)
                ins.then_inc(g_mm, 1)

            pe.wait_ge(in_gate, 16)
            for u in range(2):
                waits_scores2(u)
                for n in range(8):
                    ins = score2(u, n)
                ins.then_inc(s2_mm, 1)
            for u in range(2 * B):
                unit(u)
                if u == 2:
                    turn_out(0)
                if u == 3:
                    out_project(0)
                    turn_out(1)
                if u == 5:
                    turn_gate(0)
                    out_project(1)
                    turn_out(2)
                if u == 6:
                    out_project(2)
                    turn_gate(1)
            turn_out(3)
            gate_project(0, 2 * B)
            gate_project(1, 2 * B)
            out_project(3)
            turn_gate(2)
            gate_project(2, 2 * B)
            turn_gate(3)
            gate_project(3, 2 * B)
            pe.wait_ge(g_ok, 1)
            nc.tensor.transpose(pv[0:B * E, 0:T], gsm[:, 3], ident[:]).then_inc(pt_g, 1)
            pe.wait_ge(slot_ok, 1)
            nc.tensor.transpose(pk[:, 0:B * E], chosen[:, 2], ident[0:B * E, 0:B * E]).then_inc(slot_mm, 1)
            pe.wait_ge(onehot_ok, 1)
            pe.wait_ge(norm_lo_ok, B)
            for c in range(8):
                k, pair = c % 4, c // 4
                for b in (2 * pair, 2 * pair + 1):
                    for part in (norm_hi, norm_lo):
                        ins = mm(banks[c][:, (b % 2) * E * CAP:(b % 2 + 1) * E * CAP], part[:, b, k * P:(k + 1) * P],
                                 onehot[:, b].rearrange("p e s -> p (e s)"), start=part is norm_hi, stop=part is norm_lo,
                                 skip_group_check=True)
                ins.then_inc(xin_mm, 1)
            pe.wait_ge(weighted_ok, 1)
            pe.wait_ge(xin_dve, 4)
            pe.wait_ge(xin_act, 4)
            for e in range(E):
                ins = nc.tensor.transpose((pk, pv)[e // 4][:, (e % 4) * T:(e % 4 + 1) * T], weighted[:, e].rearrange("p b s -> p (b s)"), ident[:])
                if e % 4 == 3:
                    ins.then_inc(back_mm, 1)
            pe.wait_ge(back_ok, 4)

            def passes(dst, left_hi, left_lo, slot, q, start):
                terms = [(l[:, c], r[:, slot, c - q]) for c in range(q, q + KC)
                         for l, r in ((left_hi, w_hi), (left_hi, w_lo), (left_lo, w_hi))]
                for i, (l, r) in enumerate(terms):
                    ins = mm(dst, l, r, start=start and i == 0, stop=i == len(terms) - 1, skip_group_check=True)
                return ins

            def hidden(e, q):
                if q == 0:
                    pe.wait_ge(xin_staged, e + 1)
                pe.wait_ge(lo_ok, SLOTS if isinstance(e, int) and e == 0 else e * 8 + (q + 1))
                if q >= 2 or not isinstance(e, int):
                    pe.wait_ge(gelu_ok, e * 4 + (q - 1))
                passes((pk, pv)[q % 2][:], xin_hi, xin_lo, q % SLOTS, 0, True).then_inc(tile_mm, 1)

            def turn(e, q):
                pe.wait_ge(gelu_ok, e * 4 + (q + 1))
                if q or not isinstance(e, int):
                    pe.wait_ge(ht_lo_ok, e * 4 + q)
                for c in range(KC):
                    ins = nc.tensor.transpose(po[:, 1, c * P:(c + 1) * P], h_s[:, q % 2, c * P:(c + 1) * P], ident[:])
                ins.then_inc(ht_mm, 1)

            def expert_out(e, q):
                pe.wait_ge(lo_ok, e * 8 + (NQ + q + 1))
                pe.wait_ge(ht_lo_ok, e * 4 + (q + 1))
                if q == 0 and not isinstance(e, int):
                    pe.wait_ge(y_ok, e)
                passes(po[:, 0], ht_hi, ht_lo, q % SLOTS, q * KC, q == 0).then_inc(tile_mm, 1)

            def scatter(e):
                pe.wait_ge(back_staged, e + 1)
                pe.wait_ge(y_lo_ok, e + 1)
                first = isinstance(e, int) and e == 0
                for b in range(B):
                    r = slice(b * CAP, (b + 1) * CAP)
                    for y in (y_hi, y_lo):
                        ins = mm(ps[:, b], back_now[r], y[r], start=first and y is y_hi, stop=False, skip_group_check=True)
                ins.then_inc(sc_mm, 1)

            def expert(e, before):
                hidden(e, 0)
                hidden(e, 1)
                turn(e, 0)
                if before is not None:
                    scatter(before)
                hidden(e, 2)
                turn(e, 1)
                hidden(e, 3)
                turn(e, 2)
                expert_out(e, 0)
                turn(e, 3)
                for q in range(1, NQ):
                    expert_out(e, q)

            expert(0, None)
            expert(1, 0)
            with pe.Fori(2, E) as e:
                expert(e, e - 1)
            scatter(E - 1)


_INS = ["x", "ctx_t", "key_bias", "key_mask", "wq", "bq", "wk", "bk", "wv", "bv", "wo", "bo",
        "sq", "sbq", "sk", "sbk", "sv", "sbv", "so", "sbo", "gate", "w1", "w2"]


def kernel(**inputs):
    import numpy as np
    import concourse.bacc as bacc
    from concourse.bass_utils import run_bass_kernel_spmd

    a = {k: np.asarray(v) for k, v in inputs.items()}

    def columns(v):
        return v.reshape(KC, P).T

    kv_w, kv_b = a["L0_xattn_Wkv_w"], a["L0_xattn_Wkv_b"]
    laid = {
        "x": a["x"],
        "ctx_t": a["ctx_1024"].reshape(NJ, P, KC, P).transpose(0, 3, 2, 1),
        "key_bias": a["fside_BxS2_0"].reshape(NJ, P),
        "key_mask": a["mask_BxS2_bk0"].reshape(NJ, P),
        "wq": a["L0_xattn_Wq_w"].T, "bq": columns(a["L0_xattn_Wq_b"]),
        "wk": kv_w[:D].T, "bk": columns(kv_b[:D]),
        "wv": kv_w[D:].T, "bv": kv_b[D:],
        "wo": a["L0_xattn_out_w"].T, "bo": a["L0_xattn_out_b"],
        "sq": a["L0_attn_Wq"].T, "sbq": columns(a["L0_attn_bq"]),
        "sk": a["L0_attn_Wk"].T, "sbk": columns(a["L0_attn_bk"]),
        "sv": a["L0_attn_Wv"].T, "sbv": a["L0_attn_bv"],
        "so": a["L0_attn_Wo"].T, "sbo": a["L0_attn_bo"],
        "gate": a["L0_ffn_gate_w"], "w1": a["L0_ffn_w1"], "w2": a["L0_ffn_w2"],
    }
    nc = bacc.Bacc("TRN2", target_bir_lowering=False, num_devices=1, dynamic_dma_scratch_size=1024)
    arrays, args = {}, []
    for name in _INS:
        v = np.ascontiguousarray(laid[name])
        arrays[f"in_{name}"] = v
        args.append(nc.dram_tensor(f"in_{name}", v.shape, mybir.dt.from_np(v.dtype), kind="ExternalInput").ap())
    args.append(nc.dram_tensor("out", (B, T, D), F32, kind="ExternalOutput").ap())
    decoder_layer(nc, *args)
    r = run_bass_kernel_spmd(nc, [arrays], core_ids=[0])
    return r.results[0]["out"]
```

```python
from contextlib import ExitStack

import concourse.bass as bass
from concourse import mybir

ALU = mybir.AluOpType
ACT = mybir.ActivationFunctionType
AX = mybir.AxisListType
F32 = mybir.dt.float32
F32R = mybir.dt.float32r
BF16 = mybir.dt.bfloat16
I32 = mybir.dt.int32
U8 = mybir.dt.uint8

P = 128
B, T, D = 4, 128, 512
SK = 2048
H, DH = 16, 32
KC = D // P
NCH = SK // P
NJ = B * NCH
STRIPS = P // DH
E, F = 8, 2048
CAP = 2 * T // E
FC = F // P
NQ = F // D
SLOTS = 4
HV = DH + 1
MASKED = 1.0e30
EPS_LN = 1e-5
LO, HI = 1e-7, 1.0 - 1e-7
SCALE = DH ** -0.5


def decoder_layer(nc, x, ctx_t, key_bias, key_mask, wq, bq, wk, bk, wv, bv, wo, bo,
                  sq, sbq, sk, sbk, sv, sbv, so, sbo, gate, w1, w2, out):
    with ExitStack() as ctx:
        def sb(name, shape, dt=F32):
            return ctx.enter_context(nc.sbuf_tensor(name, shape, dt))

        def sem(name):
            return ctx.enter_context(nc.semaphore(name))

        att_w = sb("att_w", [P, 8, KC, D])
        wq_s, wk_s, wv_s, wo_s, sq_s, sk_s, sv_s, so_s = (att_w[:, i] for i in range(8))
        q_wide = att_w[:, 6:8].rearrange("p i c (g t) -> p i c g t", g=KC)
        w_hi = sb("w_hi", [P, SLOTS, KC, D], F32R)
        w_lo = sb("w_lo", [P, SLOTS, KC, D], F32R)

        ctx_hi, ctx_lo = w_hi[:, 0, :, 0:P], w_lo[:, 0, :, 0:P]

        x_s = sb("x_s", [P, B, D])
        norm = sb("norm", [P, B, D])
        gcol = sb("gcol", [P, E])
        qk = sb("qk", [P, 2, B, KC, T])
        qt, kt2 = qk[:, 0], qk[:, 1]
        tr_gate = qt
        state = sb("state", [P, B, H, HV])
        run_max = sb("run_max", [P, B, H])
        cols = sb("cols", [P, 4, KC])
        gate_s = sb("gate_s", [P, KC, E])
        ident = sb("ident", [P, P])
        bias3 = sb("bias3", [P, P], BF16)
        ones3 = sb("ones3", [P, P], BF16)
        mc = sb("mc", [P, H])
        mnew = sb("mnew", [P, H])
        negm = sb("negm", [P, H])
        mdiff = sb("mdiff", [P, H])
        alpha = sb("alpha", [P, H])
        norm_c = sb("norm_c", [P, B, H])
        stats = sb("stats", [P, B, 6])
        aggr = sb("aggr", [P, B, 2])
        rstd = sb("rstd", [P, B])
        zero = sb("zero", [P, 1])
        minus_half = sb("minus_half", [P, B])
        table = sb("table", [1, 2 * (NJ + 1) + 1], I32)
        gsm = sb("gsm", [P, 4, B * E])
        gred = sb("gred", [P, 4, B])
        top8 = sb("top8", [B * E, 8])
        slot_t = sb("slot_t", [P, B * E])
        iota_s = sb("iota_s", [P, CAP])
        attention = ExitStack()

        def early(name, shape, dt=F32):
            return attention.enter_context(nc.sbuf_tensor(name, shape, dt))

        tr_hi = early("tr_hi", [P, KC, B * T], F32R)
        tr_lo = early("tr_lo", [P, KC, B * T], F32R)
        big_a = early("big_a", [P, H, P])
        ctx_s = early("ctx_s", [P, KC, P])
        kt_s = early("kt_s", [P, KC, P])
        q_now = early("q_now", [P, KC, T])
        values = ExitStack()
        v_s = values.enter_context(nc.sbuf_tensor("v_s", [P, B, H, HV], F32))
        values.close()
        onehot_s = early("onehot_s", [P, B * E * CAP], F32R)
        early("rest_of_v", [P, B * H * HV - B * E * CAP])
        bv_b = early("bv_b", [P, D])
        bo_b = early("bo_b", [P, D])
        start = ExitStack()

        def first(name, shape, dt=F32):
            return start.enter_context(nc.sbuf_tensor(name, shape, dt))

        mask_s = first("mask_s", [NJ, P], U8)
        kb_s = first("kb_s", [NJ, P])
        kb_m = first("kb_m", [NJ, P])
        kb_3 = first("kb_3", [NJ, 3, P], BF16)
        idx = first("idx", [NJ, 8])
        tri = first("tri", [NJ, NJ])
        slots = first("slots", [NJ, NJ + 1])
        pick = first("pick", [NJ, NJ + 1])
        start.close()
        big_b = early("big_b", [P, H, P])
        attention.close()
        x_now = sb("x_now", [P, KC, P])
        xin_hi = sb("xin_hi", [P, KC, P], F32R)
        xin_lo = sb("xin_lo", [P, KC, P], F32R)
        h_s = sb("h_s", [P, 2, D])
        ht_hi = sb("ht_hi", [P, FC, P], F32R)
        ht_lo = sb("ht_lo", [P, FC, P], F32R)
        y_s = sb("y_s", [P, D])
        y_hi = sb("y_hi", [P, D], F32R)
        y_lo = sb("y_lo", [P, D], F32R)
        back_now = sb("back_now", [P, T], F32R)
        rounded = sb("rounded", [P, B, D], BF16)

        prob_t = ctx_s[0:B * E, 0]
        work = ctx_s[0:B * E, 1:3]
        chosen = kt_s[0:B * E, 0:3]
        norm_hi, norm_lo = (t[:].rearrange("p k n -> p (k n)").rearrange("p (b n) -> p b n", b=B) for t in (tr_hi, tr_lo))
        onehot = onehot_s[:].rearrange("p (b e s) -> p b e s", b=B, e=E)
        weighted = big_a[:].rearrange("p h k -> p (h k)")[:, 0:B * E * CAP].rearrange("p (e b s) -> p e b s", b=B, e=E)
        xin = qk[:].rearrange("p i b k t -> p (i b k t)").rearrange("p (k e n) -> p k e n", k=KC, e=E)
        spare = state[:].rearrange("p b h d -> p (b h d)")
        back = spare[:, 0:E * T].rearrange("p (e t) -> p e t", e=E)

        ps = ctx.enter_context(nc.psum_tensor("ps", [P, 4, 512], F32))
        pk = ctx.enter_context(nc.psum_tensor("pk", [P, 512], F32))
        pv = ctx.enter_context(nc.psum_tensor("pv", [P, 512], F32))
        po = ctx.enter_context(nc.psum_tensor("po", [P, 2, 512], F32))
        banks = [ps[:, 0], ps[:, 1], ps[:, 2], ps[:, 3], pk[:], pv[:], po[:, 0], po[:, 1]]

        logits = po[:, 1, 8 * HV:8 * HV + B * E]

        rows3 = nc.dram_tensor("rows3", [NJ, 3, P], BF16, kind="Internal").ap()

        in_mask, in_x, in_wk, in_wv, in_bo, in_sb, in_gate, in_cols = (sem(f"in_{n}") for n in (
            "mask", "x", "wk", "wv", "bo", "sb", "gate", "cols"))
        in_wq, in_wo, in_sq, in_sk, in_sv, in_so = (sem(f"in_{n}") for n in ("wq", "wo", "sq", "sk", "sv", "so"))
        att_hi_ok = sem("att_hi_ok"); att_lo_ok = sem("att_lo_ok")
        rows_out = sem("rows_out")
        consts = sem("consts")
        act_ok = sem("act_ok"); place_mm = sem("place_mm")
        pick_ok = sem("pick_ok"); table_mm = sem("table_mm"); table_ok = sem("table_ok"); rows_ok = sem("rows_ok")
        ctx_in = sem("ctx_in"); bias_in = sem("bias_in"); ctx_hi_ok = sem("ctx_hi_ok"); ctx_lo_ok = sem("ctx_lo_ok"); k_mm = sem("k_mm"); v_mm = sem("v_mm")
        k_out = sem("k_out"); v_out = sem("v_out"); s_mm = sem("s_mm"); q_staged = sem("q_staged")
        negm_ok = sem("negm_ok"); alpha_ok = sem("alpha_ok"); p_ok = sem("p_ok"); pt_mm = sem("pt_mm")
        pt_dve = sem("pt_dve"); pt_act = sem("pt_act"); pv_mm = sem("pv_mm"); summed = sem("summed")
        loop_dve = sem("loop_dve")
        var_ok = sem("var_ok"); rstd_ok = sem("rstd_ok")
        dchain = sem("dchain"); pchain = sem("pchain")
        normed = [sem(f"normed{i}") for i in range(5)]
        tr_mm = [sem(f"tr_mm{i}") for i in range(5)]
        tr_hi_ok = [sem(f"tr_hi_ok{i}") for i in range(5)]
        tr_lo_ok = [sem(f"tr_lo_ok{i}") for i in range(4)]
        q_mm = sem("q_mm"); q_out = sem("q_out")
        o_mm = sem("o_mm"); o_out = sem("o_out")
        q2_mm = sem("q2_mm"); k2_mm = sem("k2_mm"); v2_mm = sem("v2_mm")
        wide_ok = sem("wide_ok"); norm_hi_ok = sem("norm_hi_ok"); norm_lo_ok = sem("norm_lo_ok"); cleared = sem("cleared")
        q2_act = sem("q2_act"); q2_out = sem("q2_out"); k2_out = sem("k2_out"); v2_out = sem("v2_out")
        s2_mm = sem("s2_mm"); s2_clamped = sem("s2_clamped"); e2_ok = sem("e2_ok"); pv2_mm = sem("pv2_mm"); pv2_out = sem("pv2_out")
        o2_mm = sem("o2_mm"); o2_out = sem("o2_out")
        g_mm = sem("g_mm"); g_sub = sem("g_sub"); g_exp = sem("g_exp"); g_ok = sem("g_ok"); pt_g = sem("pt_g")
        slot_ok = sem("slot_ok"); slot_mm = sem("slot_mm"); onehot_ok = sem("onehot_ok"); weighted_ok = sem("weighted_ok")
        xin_mm = sem("xin_mm"); xin_dve = sem("xin_dve"); xin_act = sem("xin_act")
        back_mm = sem("back_mm"); back_ok = sem("back_ok")
        raw_in = [sem(f"raw_in{i}") for i in range(2 * NQ)]
        hi_ok = sem("hi_ok"); lo_ok = sem("lo_ok")
        tile_mm = sem("tile_mm")
        x_now_ok = sem("x_now_ok"); xin_hi_ok = sem("xin_hi_ok"); xin_staged = sem("xin_staged"); back_staged = sem("back_staged")
        gelu_ok = sem("gelu_ok"); ht_mm = sem("ht_mm"); ht_hi_ok = sem("ht_hi_ok"); ht_lo_ok = sem("ht_lo_ok")
        y_ok = sem("y_ok"); y_hi_ok = sem("y_hi_ok"); y_lo_ok = sem("y_lo_ok"); sc_mm = sem("sc_mm")
        rounded_ok = sem("rounded_ok"); summed_up = sem("summed_up"); res_ok = sem("res_ok"); stored = sem("stored")

        SPLITS = ((wq_s, 2, in_wq), (wv_s, 1, in_wv), (sq_s, 3, in_sq), (wo_s, 2, in_wo), (sv_s, 1, in_sv), (sk_s, 0, in_sk), (so_s, 3, in_so))
        TURN_BANKS = [[0, 1, 2, 3], [4, 5, 6, 7], [0, 1, 2, 6], [4] * 4, [4] * 4]
        V2_BANKS = [3, 0, 1, 4]
        CROSS_BANKS = [4, 5, 4, 5]

        def turned(i, b):
            return banks[TURN_BANKS[i][b]].rearrange("p (k t) -> p k t", k=KC)

        def of_batch(tensor, b):
            return tensor[:, :, b * T:(b + 1) * T]

        def chunk_j(eng, t):
            return eng.value_load(table[0:1, bass.ds(t, 1)], min_val=0, max_val=NJ - 1)

        def chunk_b(eng, t):
            return eng.value_load(table[0:1, bass.ds(t + (NJ + 1), 1)], min_val=0, max_val=B - 1)

        def last_chunk(eng):
            eng.wait_ge(table_ok, 2)
            return eng.value_load(table[0:1, 2 * (NJ + 1):2 * (NJ + 1) + 1], min_val=B - 1, max_val=NJ - 1)

        def w_tile(e, i):
            if i < NQ:
                w = w1[bass.ds(e, 1), :, i * D:(i + 1) * D]
            else:
                w = w2[bass.ds(e, 1), (i - NQ) * D:(i - NQ + 1) * D, :]
            return w.rearrange("a (k p) n -> p (a k) n", p=P)

        def prime(eng, *sems):
            for s in sems:
                eng.sem_inc(s, 1)

        block = ctx.enter_context(nc.Block())

        @block.sync
        def _(sp):
            sp.dma_start(mask_s[:], key_mask).then_inc(in_mask, 16)
            sp.dma_start(kb_s[:], key_bias).then_inc(in_mask, 16)
            sp.dma_start(x_s[:], x.rearrange("b t d -> t b d")).then_inc(in_x, 16)
            sp.dma_start(wk_s, wk.rearrange("(k p) n -> p k n", p=P)).then_inc(in_wk, 16)
            for i, v in enumerate((bq, bk, sbq, sbk)):
                sp.dma_start(cols[:, i, :], v).then_inc(in_cols, 16)
            sp.dma_start(bv_b[:], bv.partition_broadcast(P)).then_inc(in_cols, 16)
            sp.dma_start(wq_s, wq.rearrange("(k p) n -> p k n", p=P)).then_inc(in_wq, 16)

            def load_chunk(t):
                j = chunk_j(sp, t)
                sp.dma_start(ctx_s[:], ctx_t[bass.ds(j, 1)].rearrange("a p k n -> (a p) k n")).then_inc(ctx_in, 16)

            def load_bias(t):
                j = chunk_j(sp, t)
                sp.wait_ge(s_mm, t + 1)
                sp.dma_start(bias3[0:3, :], rows3[bass.ds(j, 1)].rearrange("a r n -> (a r) n")).then_inc(bias_in, 16)

            last = last_chunk(sp)
            load_chunk(0)
            sp.dma_start(wv_s, wv.rearrange("(k p) n -> p k n", p=P)).then_inc(in_wv, 16)
            sp.wait_ge(rows_ok, 1)
            sp.dma_start(rows3, kb_3[:]).then_inc(rows_out, 16)
            sp.wait_ge(rows_out, 16)
            sp.wait_ge(consts, 6)
            with sp.Fori(0, last) as t:
                load_bias(t)
                sp.wait_ge(k_mm, t + 1)
                sp.wait_ge(ctx_lo_ok, t + 1)
                load_chunk(t + 1)
            load_bias(last)
            sp.wait_ge(v_out, last + 1)
            sp.dma_start(bv_b[:], sbv.partition_broadcast(P)).then_inc(in_sb, 16)
            sp.dma_start(bo_b[:], sbo.partition_broadcast(P)).then_inc(in_sb, 16)
            sp.wait_ge(v_mm, last + 2)
            sp.wait_ge(att_lo_ok, 4)
            for i in range(2 * NQ):
                if i == 5:
                    sp.wait_ge(att_lo_ok, 6)
                if i == 6:
                    sp.wait_ge(s2_mm, 2 * B)
                sp.dma_start(att_w[:, i], w_tile(0, i)).then_inc(raw_in[i], 16)
            sp.wait_ge(lo_ok, SLOTS)
            with sp.Fori(1, E) as e:
                for i in range(2 * NQ):
                    sp.wait_ge(lo_ok, e * 8 + (i - 7))
                    sp.dma_start(att_w[:, i], w_tile(e, i)).then_inc(raw_in[i], 16)
            for b in range(B):
                sp.wait_ge(res_ok, b + 1)
                sp.dma_start(out[b], x_s[:, b]).then_inc(stored, 16)
            sp.wait_ge(stored, 16 * B)

        @block.gpsimd
        def _(pool):
            g = nc.gpsimd

            def inverse_roots(n):
                for b in range(B):
                    pool.wait_ge(var_ok, n * B + b + 1)
                    g.tensor_tensor(rstd[:, b:b + 1], rstd[:, b:b + 1], minus_half[:, b:b + 1], ALU.pow).then_inc(rstd_ok, 1)

            g.memset(ident[:], 0.0).then_inc(pchain, 1)
            g.memset(minus_half[:], -0.5).then_inc(pchain, 1)
            g.memset(zero[:], 0.0).then_inc(pchain, 1)
            g.memset(tri[:], 1.0).then_inc(pchain, 1)
            g.memset(ones3[:], 0.0).then_inc(pchain, 1)
            g.iota(idx[:, 0:1], pattern=[[0, 1]], base=0, channel_multiplier=1,
                   allow_small_or_imprecise_dtypes=True).then_inc(consts, 1)
            g.iota(slots[:], pattern=[[1, NJ + 1]], base=0, channel_multiplier=0,
                   allow_small_or_imprecise_dtypes=True).then_inc(consts, 1)
            g.iota(iota_s[:], pattern=[[1, CAP]], base=1, channel_multiplier=0,
                   allow_small_or_imprecise_dtypes=True).then_inc(consts, 1)
            pool.wait_ge(pchain, 5)
            g.affine_select(out=ident[:], in_=ident[:], compare_op=ALU.not_equal, fill=1.0, base=0,
                            pattern=[[-1, P]], channel_multiplier=1).then_inc(consts, 1)
            g.affine_select(out=tri[:], in_=tri[:], compare_op=ALU.is_gt, fill=0.0, base=0,
                            pattern=[[1, NJ]], channel_multiplier=-1).then_inc(consts, 1)
            g.memset(bias3[:], 0.0).then_inc(consts, 1)
            g.memset(ones3[0:3, :], 1.0).then_inc(consts, 1)
            g.memset(idx[:, 5:6], 1.0).then_inc(consts, 1)
            g.memset(v_s[:, :, :, DH:HV], 1.0).then_inc(consts, 1)
            g.memset(state[:], 0.0).then_inc(consts, 1)
            g.memset(run_max[:], -MASKED).then_inc(consts, 1)
            inverse_roots(0)
            last = last_chunk(pool)
            pool.wait_ge(q_out, 4)
            with pool.Fori(1, last + 1) as t:
                b = chunk_b(pool, t)
                pool.wait_ge(s_mm, t + 1)
                g.tensor_copy(q_now[:], qt[:, bass.ds(b, 1)].rearrange("p a k n -> p (a k) n")).then_inc(q_staged, 1)
            pool.wait_ge(in_sv, 16)
            pool.wait_ge(v_mm, last + 2)
            pool.wait_ge(s_mm, last + 2)
            pool.wait_ge(q_staged, last + 1)
            g.tensor_tensor(w_hi[:, 1], sv_s, zero[:].unsqueeze(2).broadcast_to([P, KC, D]), ALU.add).then_inc(att_hi_ok, 1)
            pool.wait_ge(att_hi_ok, 5)
            g.tensor_tensor(w_lo[:, 1], sv_s, w_hi[:, 1], ALU.subtract).then_inc(att_lo_ok, 1)
            pool.wait_ge(att_lo_ok, 5)
            inverse_roots(1)
            for i in range(2):
                pool.wait_ge(att_lo_ok, 5 + 2 * i)
                g.memset(att_w[:, 6 + i], 0.0).then_inc(cleared, 1)
            inverse_roots(2)
            pool.wait_ge(o2_mm, B)
            for b in range(B):
                pool.wait_ge(norm_hi_ok, b + 1)
                if b:
                    pool.wait_ge(norm_lo_ok, b)
                g.tensor_tensor(norm_lo[:, b], norm[:, b], norm_hi[:, b], ALU.subtract).then_inc(norm_lo_ok, 1)
            pool.wait_ge(norm_lo_ok, B)
            pool.wait_ge(raw_in[3], 16)
            pool.wait_ge(lo_ok, 3)
            g.tensor_copy(w_hi[:, 3], att_w[:, 3]).then_inc(hi_ok, 1)
            pool.wait_ge(hi_ok, 4)
            g.tensor_tensor(w_lo[:, 3], att_w[:, 3], w_hi[:, 3], ALU.subtract).then_inc(lo_ok, 1)
            pool.wait_ge(lo_ok, 4)

            def stage_input(e):
                pool.wait_ge(tile_mm, e * 8 - 4)
                now = xin[:, :, bass.ds(e, 1)].rearrange("p k a n -> p (k a) n")
                g.tensor_copy(x_now[:], now).then_inc(x_now_ok, 1)
                g.tensor_copy(xin_hi[:], now).then_inc(x_now_ok, 1)
                pool.wait_ge(x_now_ok, e * 2)
                g.tensor_tensor(xin_lo[:], x_now[:], xin_hi[:], ALU.subtract).then_inc(xin_staged, 1)

            def stage_back(e):
                g.tensor_copy(back_now[:], back[:, bass.ds(e, 1), :].rearrange("p a n -> p (a n)")).then_inc(back_staged, 1)

            pool.wait_ge(back_ok, 4)
            stage_back(0)
            with pool.Fori(1, E) as e:
                stage_input(e)
                pool.wait_ge(sc_mm, e)
                stage_back(e)

        @block.scalar
        def _(act):
            a = nc.scalar
            prime(act, pt_act)

            def split_att(n):
                w, slot, landed = SPLITS[n]
                act.wait_ge(landed, 16)
                a.copy(w_hi[:, slot], w).then_inc(att_hi_ok, 1)

            def transposed(i, b):
                act.wait_ge(tr_mm[i], b + 1)
                a.copy(of_batch(tr_hi, b), turned(i, b)).then_inc(tr_hi_ok[i], 1)

            def k_evacuate(t):
                act.wait_ge(k_mm, t + 1)
                for c in range(KC):
                    ins = a.activation(kt_s[:, c], pk[:, c * P:(c + 1) * P], ACT.Identity, bias=cols[:, 1, c:c + 1])
                ins.then_inc(k_out, 1)

            def softmax_chunk(t, more):
                act.wait_ge(negm_ok, 2 * t + 2)
                act.wait_ge(summed, t + 1)
                a.activation(alpha[:], mdiff[:], ACT.Exp).then_inc(alpha_ok, 1)
                for c in range(STRIPS):
                    for g in range(KC):
                        h = c * KC + g
                        ins = a.activation(big_a[:, h], ps[:, c, g * P:(g + 1) * P], ACT.Exp, bias=negm[:, h:h + 1])
                    ins.then_inc(p_ok, 1)
                if more:
                    k_evacuate(t + 1)
                act.wait_ge(pt_mm, 4 * t + 4)
                a.copy(big_b[:, 3 * KC:4 * KC].rearrange("p h k -> p (h k)"), ps[:, 3]).then_inc(pt_act, 1)

            last = last_chunk(act)
            split_att(0)
            for b in range(B):
                transposed(0, b)
            act.dma_start(wo_s, wo.rearrange("(k p) n -> p k n", p=P)).then_inc(in_wo, 16)
            act.dma_start(bo_b[:], bo.partition_broadcast(P)).then_inc(in_bo, 16)
            for w, s, landed in ((sq, sq_s, in_sq), (sv, sv_s, in_sv), (sk, sk_s, in_sk), (so, so_s, in_so)):
                act.dma_start(s, w.rearrange("(k p) n -> p k n", p=P)).then_inc(landed, 16)
            act.dma_start(gate_s[:], gate.rearrange("(k p) e -> p k e", p=P)).then_inc(in_gate, 16)

            def split_chunk(t):
                act.wait_ge(ctx_in, t * 16 + 16)
                act.wait_ge(v_mm, t + 1)
                a.copy(ctx_hi, ctx_s[:]).then_inc(ctx_hi_ok, 1)

            split_chunk(0)
            split_att(1)
            act.wait_ge(in_cols, 80)
            k_evacuate(0)
            split_att(2)
            act.wait_ge(q_mm, KC)
            split_att(3)
            with act.Fori(0, last) as t:
                split_chunk(t + 1)
                softmax_chunk(t, True)
            for b in range(B - 1):
                transposed(1, b)
            softmax_chunk(last, False)
            transposed(2, 0)
            transposed(1, 3)
            for b in range(1, B):
                transposed(2, b)
            act.wait_ge(att_lo_ok, 5)
            split_att(5)
            for c in range(KC):
                act.wait_ge(q2_mm, c + 1)
                a.activation(qt[:, :, c], banks[4 + c].rearrange("p (b t) -> p b t", b=B), ACT.Identity,
                             bias=cols[:, 2, c:c + 1]).then_inc(q2_act, 1)
            split_att(6)

            def split_first(i, used):
                act.wait_ge(raw_in[i], 16)
                act.wait_ge(used, KC)
                a.copy(w_hi[:, i], att_w[:, i]).then_inc(hi_ok, 1)

            def widen(b):
                act.wait_ge(q2_out, KC)
                act.wait_ge(cleared, min(b, 1) + 1)
                if b >= 2:
                    act.wait_ge(s2_mm, 2 * b - 2)
                for c in range(STRIPS):
                    r = slice(c * DH, (c + 1) * DH)
                    a.copy(q_wide[r, b % 2, c], qt[r, b]).then_inc(wide_ok, 1)

            for c in range(KC):
                act.wait_ge(k2_mm, c + 1)
                a.activation(kt2[:, :, c], ps[:, c].rearrange("p (b t) -> p b t", b=B), ACT.Identity,
                             bias=cols[:, 3, c:c + 1]).then_inc(q2_act, 1)
                if c == 1:
                    split_first(2, o_mm)
                else:
                    if c < 3:
                        widen(c // 2)
            split_first(0, k2_mm)

            def exps2(u):
                half = big_a if u % 2 == 0 else big_b
                act.wait_ge(s2_clamped, u + 1)
                if u >= 2:
                    act.wait_ge(pv2_mm, u - 1)
                a.activation(half[:, 8:16], half[:, 0:8], ACT.Exp).then_inc(e2_ok, 1)

            def gate_transposed(b):
                act.wait_ge(tr_mm[4], b + 1)
                a.copy(tr_gate[:, b], turned(4, b)).then_inc(tr_hi_ok[4], 1)

            exps2(0)
            exps2(1)
            widen(2)
            split_first(1, v2_mm)
            for u in range(2 * B):
                if u + 2 < 2 * B:
                    exps2(u + 2)
                if u == 1:
                    widen(3)
                if u == 2:
                    transposed(3, 0)
                if u == 3:
                    transposed(3, 1)
                if u == 5:
                    gate_transposed(0)
                    transposed(3, 2)
                if u == 6:
                    gate_transposed(1)
            transposed(3, B - 1)
            gate_transposed(2)
            for b in range(B):
                if b == B - 1:
                    gate_transposed(3)
                act.wait_ge(normed[4], b + 1)
                a.copy(norm_hi[:, b], norm[:, b]).then_inc(norm_hi_ok, 1)
            act.wait_ge(g_sub, 1)
            a.activation(gsm[:, 2], gsm[:, 1], ACT.Exp).then_inc(g_exp, 1)
            for i in range(4):
                c = 2 * i + 1
                act.wait_ge(xin_mm, c + 1)
                a.copy(xin[:, c % 4].rearrange("p e (b s) -> p b e s", b=B)[:, 2 * (c // 4):2 * (c // 4) + 2],
                       banks[c].rearrange("p (b e s) -> p b e s", b=2, e=E)).then_inc(xin_act, 1)
            act.wait_ge(xin_dve, 4)
            act.wait_ge(xin_act, 4)
            a.copy(xin_hi[:], xin[:, :, 0]).then_inc(xin_hi_ok, 1)

            def split_hi(e, i):
                act.wait_ge(raw_in[i], e * 16 + 16)
                act.wait_ge(tile_mm, e * 8 + (i - SLOTS + 1))
                a.copy(w_hi[:, i % SLOTS], att_w[:, i]).then_inc(hi_ok, 1)

            def gelu(e, q):
                act.wait_ge(tile_mm, e * 8 + (q + 1))
                if q >= 2 or not isinstance(e, int):
                    act.wait_ge(ht_mm, e * 4 + (q - 1))
                a.activation(h_s[:, q % 2], (pk, pv)[q % 2][:], ACT.Gelu_apprx_tanh).then_inc(gelu_ok, 1)

            def transposed_hi(e, q):
                act.wait_ge(ht_mm, e * 4 + (q + 1))
                a.copy(ht_hi[:, q * 4:q * 4 + 4].rearrange("p c n -> p (c n)"), po[:, 1]).then_inc(ht_hi_ok, 1)

            def expert(e, more):
                gelu(e, 0)
                split_hi(e, 4)
                gelu(e, 1)
                transposed_hi(e, 0)
                split_hi(e, 5)
                gelu(e, 2)
                transposed_hi(e, 1)
                split_hi(e, 6)
                gelu(e, 3)
                transposed_hi(e, 2)
                split_hi(e, 7)
                transposed_hi(e, 3)
                if more:
                    for i in range(SLOTS):
                        split_hi(e + 1, i)
                act.wait_ge(y_ok, e + 1)
                if not isinstance(e, int) or e > 0:
                    act.wait_ge(sc_mm, e)
                a.copy(y_hi[:], y_s[:]).then_inc(y_hi_ok, 1)

            expert(0, True)
            with act.Fori(1, E - 1) as e:
                expert(e, True)
            expert(E - 1, False)
            for b in range(B):
                act.wait_ge(summed_up, b + 1)
                a.copy(rounded[:, b], ps[:, b]).then_inc(rounded_ok, 1)

        @block.vector
        def _(dve):
            v = nc.vector
            links = [0]
            ln_count = [0]

            def link(ins):
                ins.then_inc(dchain, 1)
                links[0] += 1
                dve.wait_ge(dchain, links[0])

            def statistics(b):
                link(v.bn_stats(stats[:, b], x_s[:, b]))
                link(v.bn_aggr(aggr[:, b], stats[:, b]))
                v.tensor_scalar(rstd[:, b:b + 1], aggr[:, b, 1:2], EPS_LN, None, ALU.add).then_inc(var_ok, 1)

            def normed_batch(i, b):
                ln_count[0] += 1
                dve.wait_ge(rstd_ok, ln_count[0])
                v.tensor_scalar(norm[:, b], x_s[:, b], aggr[:, b, 0:1], rstd[:, b:b + 1],
                                ALU.subtract, ALU.mult).then_inc(normed[i], 1)

            def transposed(i, b):
                dve.wait_ge(tr_hi_ok[i], b + 1)
                v.tensor_tensor(of_batch(tr_lo, b), turned(i, b), of_batch(tr_hi, b), ALU.subtract).then_inc(tr_lo_ok[i], 1)

            def split_att(n):
                w, slot, _ = SPLITS[n]
                dve.wait_ge(att_hi_ok, n + 1)
                v.tensor_tensor(w_lo[:, slot], w, w_hi[:, slot], ALU.subtract).then_inc(att_lo_ok, 1)

            def heads(ap):
                return ap.rearrange("p (g j d) -> p j g d", j=STRIPS, d=DH)

            prime(dve, summed, pt_dve)
            dve.wait_ge(in_mask, 32)
            dve.wait_ge(consts, 11)
            v.tensor_reduce(idx[:, 3:4], mask_s[:], AX.X, ALU.max)
            link(v.tensor_scalar(idx[:, 2:3], idx[:, 0:1], float(NCH), None, ALU.is_ge))
            for b in range(2, B):
                link(v.scalar_tensor_tensor(idx[:, 2:3], idx[:, 0:1], float(b * NCH), idx[:, 2:3], ALU.is_ge, ALU.add))
            link(v.scalar_tensor_tensor(idx[:, 1:2], idx[:, 2:3], -float(NCH), idx[:, 0:1], ALU.mult, ALU.add))
            link(v.tensor_scalar(idx[:, 6:7], idx[:, 1:2], float(NCH - 1), None, ALU.is_equal))
            v.tensor_tensor(idx[:, 7:8], idx[:, 3:4], idx[:, 6:7], ALU.max).then_inc(act_ok, 1)
            dve.wait_ge(in_x, 16)
            statistics(0)
            statistics(1)
            dve.wait_ge(place_mm, 1)
            link(v.tensor_copy(idx[:, 4:5], pv[0:NJ, 0:1]))
            v.tensor_scalar(pick[:], slots[:], idx[:, 4:5], idx[:, 7:8], ALU.is_equal, ALU.mult).then_inc(pick_ok, 1)
            statistics(2)
            dve.wait_ge(table_mm, 1)
            n_at = 2 * (NJ + 1)
            v.tensor_copy(table[:, 0:n_at], pv[0:1, 0:n_at]).then_inc(table_ok, 1)
            v.tensor_scalar(table[:, n_at:n_at + 1], pv[0:1, n_at:n_at + 1], -1.0, None, ALU.add).then_inc(table_ok, 1)

            statistics(3)
            for b in range(B):
                normed_batch(0, b)
            link(v.tensor_scalar(kb_m[:], mask_s[:], 1.0, MASKED, ALU.subtract, ALU.mult))
            link(v.tensor_tensor(kb_m[:], kb_m[:], kb_s[:], ALU.add))
            link(v.tensor_copy(kb_3[:, 0], kb_m[:]))
            link(v.tensor_tensor(kb_m[:], kb_m[:], kb_3[:, 0], ALU.subtract))
            link(v.tensor_copy(kb_3[:, 1], kb_m[:]))
            link(v.tensor_tensor(kb_m[:], kb_m[:], kb_3[:, 1], ALU.subtract))
            v.tensor_copy(kb_3[:, 2], kb_m[:]).then_inc(rows_ok, 1)
            split_att(0)
            for b in range(B):
                transposed(0, b)

            def v_evacuate(t):
                dve.wait_ge(v_mm, t + 2)
                v.tensor_tensor(v_s[:, 0].rearrange("p (j g) d -> p j g d", j=STRIPS)[:, :, :, 0:DH],
                                heads(pv[:]), heads(bv_b[:]), ALU.add).then_inc(v_out, 1)

            def split_chunk(t):
                dve.wait_ge(ctx_hi_ok, t + 1)
                v.tensor_tensor(ctx_lo, ctx_s[:], ctx_hi, ALU.subtract).then_inc(ctx_lo_ok, 1)

            split_chunk(0)
            dve.wait_ge(in_bo, 16)
            for b in range(B):
                ins = v.tensor_tensor(x_s[:, b], x_s[:, b], bo_b[:], ALU.add)
            link(ins)
            split_att(1)
            dve.wait_ge(in_cols, 80)
            for c in range(KC):
                if c == 2:
                    split_att(2)
                dve.wait_ge(q_mm, c + 1)
                v.tensor_scalar(qt[:, :, c], ps[:, c].rearrange("p (b t) -> p b t", b=B), cols[:, 0, c:c + 1],
                                SCALE, ALU.add, ALU.mult).then_inc(q_out, 1)
                ins = v.tensor_scalar(q_now[:, c], ps[:, c, 0:T], cols[:, 0, c:c + 1], SCALE, ALU.add, ALU.mult)
                if c == KC - 1:
                    ins.then_inc(q_staged, 1)
            split_att(3)
            last = last_chunk(dve)

            def running(t):
                b = chunk_b(dve, t)
                return (run_max[:, bass.ds(b, 1)].rearrange("p a h -> p (a h)"),
                        state[:, bass.ds(b, 1)].rearrange("p a h d -> p (a h) d"))

            def maxima(t, rm):
                dve.wait_ge(s_mm, t + 2)
                v.tensor_reduce(mc[:], ps[:].rearrange("p c (g k) -> p (c g) k", k=P), AX.X, ALU.max).then_inc(loop_dve, 1)
                dve.wait_ge(loop_dve, 4 * t + 1)
                v.tensor_tensor(mnew[:], mc[:], rm, ALU.max).then_inc(loop_dve, 1)
                dve.wait_ge(loop_dve, 4 * t + 2)
                v.tensor_scalar(negm[:], mnew[:], -1.0, None, ALU.mult).then_inc(negm_ok, 1)
                v.tensor_tensor(mdiff[:], rm, mnew[:], ALU.subtract).then_inc(negm_ok, 1)
                dve.wait_ge(negm_ok, 2 * t + 2)
                v.tensor_tensor(rm, mc[:], rm, ALU.max).then_inc(loop_dve, 1)

            def rescale(t, st):
                dve.wait_ge(alpha_ok, t + 1)
                v.tensor_tensor(st, st, alpha[:].unsqueeze(2).broadcast_to([P, H, HV]), ALU.mult).then_inc(loop_dve, 1)

            def turned_probs(t, c):
                dve.wait_ge(pt_mm, 4 * t + c + 1)
                v.tensor_copy(big_b[:, c * KC:(c + 1) * KC].rearrange("p h k -> p (h k)"), ps[:, c]).then_inc(pt_dve, 1)

            def add_values(t, st):
                dve.wait_ge(pv_mm, t + 1)
                dve.wait_ge(loop_dve, 4 * t + 4)
                for c in range(2):
                    half = st[:, 8 * c:8 * c + 8]
                    ins = v.tensor_tensor(half, half, po[:, c, 0:8 * HV].rearrange("p (h d) -> p h d", d=HV), ALU.add)
                ins.then_inc(summed, 1)

            with dve.Fori(0, last) as t:
                v_evacuate(t)
                split_chunk(t + 1)
                rm, st = running(t)
                maxima(t, rm)
                rescale(t, st)
                for c in range(3):
                    turned_probs(t, c)
                add_values(t, st)

            def reciprocals(first, end):
                now = slice(first, end)
                link(v.tensor_scalar(norm_c[:, now], run_max[:, now], -0.1 * MASKED, None, ALU.is_gt))
                link(v.tensor_tensor(run_max[:, now], norm_c[:, now], state[:, now, :, DH], ALU.mult))
                link(v.reciprocal(run_max[:, now], run_max[:, now]))
                link(v.tensor_tensor(norm_c[:, now], norm_c[:, now], run_max[:, now], ALU.mult))

            def attended(b):
                v.tensor_tensor(heads(norm[:, b]), state[:, b].rearrange("p (j g) d -> p j g d", j=STRIPS)[:, :, :, 0:DH],
                                norm_c[:, b].rearrange("p (j g) -> p j g", j=STRIPS).unsqueeze(3).broadcast_to([P, STRIPS, KC, DH]),
                                ALU.mult).then_inc(normed[1], 1)

            def cross_output(b):
                dve.wait_ge(o_mm, b + 1)
                ins = v.tensor_tensor(x_s[:, b], x_s[:, b], banks[CROSS_BANKS[b]], ALU.add)
                ins.then_inc(o_out, 1)
                dve.wait_ge(o_out, b + 1)
                statistics(b)

            dve.wait_ge(summed, last + 1)
            reciprocals(0, B - 1)
            for b in range(B - 1):
                attended(b)
            v_evacuate(last)
            transposed(1, 0)
            rm, st = running(last)
            maxima(last, rm)
            transposed(1, 1)
            transposed(1, 2)
            rescale(last, st)
            turned_probs(last, 0)
            turned_probs(last, 1)
            cross_output(0)
            turned_probs(last, 2)
            normed_batch(2, 0)
            cross_output(1)
            add_values(last, st)
            dve.wait_ge(summed, last + 2)
            reciprocals(B - 1, B)
            attended(B - 1)
            transposed(2, 0)
            normed_batch(2, 1)
            cross_output(2)
            transposed(1, B - 1)
            normed_batch(2, 2)
            transposed(2, 1)
            cross_output(3)
            transposed(2, 2)
            normed_batch(2, 3)

            def values_out(b):
                dst = v_s[:, b].rearrange("p (j g) d -> p j g d", j=STRIPS)[:, :, :, 0:DH]
                dve.wait_ge(v2_mm, b + 1)
                link(v.tensor_tensor(dst, heads(banks[V2_BANKS[b]]), heads(bv_b[:]), ALU.add))
                v.tensor_scalar(dst, dst, LO, HI, ALU.max, ALU.min).then_inc(v2_out, 1)

            dve.wait_ge(in_sb, 32)
            values_out(0)
            transposed(2, 3)
            values_out(1)
            values_out(2)
            split_att(5)
            for c in range(KC):
                dve.wait_ge(q2_act, c + 1)
                link(v.tensor_scalar(qt[:, :, c], qt[:, :, c], SCALE, LO, ALU.mult, ALU.max))
                v.tensor_scalar(qt[:, :, c], qt[:, :, c], HI, None, ALU.min).then_inc(q2_out, 1)

            def split_first(n, i):
                dve.wait_ge(hi_ok, n + 1)
                v.tensor_tensor(w_lo[:, i], att_w[:, i], w_hi[:, i], ALU.subtract).then_inc(lo_ok, 1)

            split_att(6)
            for c in range(KC):
                dve.wait_ge(q2_act, KC + c + 1)
                v.tensor_scalar(kt2[:, :, c], kt2[:, :, c], LO, HI, ALU.max, ALU.min).then_inc(k2_out, 1)
                if c == 1:
                    split_first(0, 2)
            values_out(B - 1)

            def clamp_scores(u):
                half = big_a if u % 2 == 0 else big_b
                dve.wait_ge(s2_mm, u + 1)
                if u >= 2:
                    dve.wait_ge(e2_ok, u - 1)
                v.tensor_scalar(half[:, 0:8].rearrange("p h k -> p (h k)"),
                                ps[:, 2 * (u % 2):2 * (u % 2) + 2].rearrange("p c n -> p (c n)"),
                                LO, HI, ALU.max, ALU.min).then_inc(s2_clamped, 1)

            def normalise(u):
                b, c = u // 2, u % 2
                o3 = po[:, c, 0:8 * HV].rearrange("p (h d) -> p h d", d=HV)
                dve.wait_ge(pv2_mm, u + 1)
                if u:
                    dve.wait_ge(pv2_out, u)
                link(v.reciprocal(mc[:, 0:8], o3[:, :, DH]))
                dst = heads(norm[:, b])[:, 2 * c:2 * c + 2]
                ins = v.tensor_tensor(dst, o3[:, :, 0:DH].rearrange("p (j g) d -> p j g d", j=2),
                                      mc[:, 0:8].rearrange("p (j g) -> p j g", j=2).unsqueeze(3).broadcast_to([P, 2, KC, DH]),
                                      ALU.mult)
                ins.then_inc(pv2_out, 1)
                if c == 1:
                    dve.wait_ge(pv2_out, u + 1)
                    v.tensor_scalar(norm[:, b], norm[:, b], LO, HI, ALU.max, ALU.min).then_inc(normed[3], 1)

            def self_bias(b):
                dve.wait_ge(o2_mm, b + 1)
                link(v.tensor_tensor(norm[:, b], pv[:], bo_b[:], ALU.add))
                v.tensor_scalar(norm[:, b], norm[:, b], LO, HI, ALU.max, ALU.min).then_inc(o2_out, 1)

            def self_residual(b):
                dve.wait_ge(o2_out, b + 1)
                link(v.tensor_tensor(x_s[:, b], x_s[:, b], norm[:, b], ALU.add))
                statistics(b)

            clamp_scores(0)
            clamp_scores(1)
            split_first(1, 0)
            for u in range(2 * B):
                normalise(u)
                if u == 7:
                    self_residual(2)
                if u + 2 < 2 * B:
                    clamp_scores(u + 2)
                if u == 2:
                    transposed(3, 0)
                if u in (3, 5):
                    b = u // 2 - 1
                    self_bias(b)
                    transposed(3, b + 1)
                    self_residual(b)
                    normed_batch(4, b)
                if u == 6:
                    self_bias(2)
                if u == 0:
                    split_first(2, 1)
            transposed(3, 3)
            normed_batch(4, 2)
            self_bias(3)
            self_residual(3)
            normed_batch(4, 3)
            def by_batch(i):
                return gsm[:, i].rearrange("p (b e) -> p b e", b=B)

            def wide(i):
                return gred[:, i].unsqueeze(2).broadcast_to([P, B, E])

            g_psum = logits[:].rearrange("p (b e) -> p b e", b=B)
            dve.wait_ge(g_mm, B)
            link(v.tensor_reduce(gred[:, 0], g_psum, AX.X, ALU.max))
            v.tensor_tensor(by_batch(1), g_psum, wide(0), ALU.subtract).then_inc(g_sub, 1)
            dve.wait_ge(g_exp, 1)
            link(v.tensor_reduce(gred[:, 1], by_batch(2), AX.X, ALU.add))
            link(v.reciprocal(gred[:, 2], gred[:, 1]))
            v.tensor_tensor(by_batch(3), by_batch(2), wide(2), ALU.mult).then_inc(g_ok, 1)
            dve.wait_ge(pt_g, 1)
            link(v.tensor_copy(prob_t, pv[0:B * E, 0:T]))
            src = prob_t
            for r in range(CAP // 8):
                link(v.max(top8[:], src))
                link(v.match_replace(work[:, r % 2], top8[:], src, -1.0))
                src = work[:, r % 2]
            link(v.tensor_scalar(chosen[:, 0], src, 0.0, None, ALU.is_lt))
            link(v.memset(chosen[:, 2], 0.0))
            link(v.tensor_tensor_scan(chosen[:, 1], chosen[:, 0], chosen[:, 2], 0.0, ALU.add, ALU.add))
            v.tensor_tensor(chosen[:, 2], chosen[:, 0], chosen[:, 1], ALU.mult).then_inc(slot_ok, 1)
            dve.wait_ge(slot_mm, 1)
            link(v.tensor_copy(slot_t[:], pk[:, 0:B * E]))
            be = "p b e s -> p (b e) s"
            v.tensor_tensor(onehot.rearrange(be), slot_t[:].unsqueeze(2).broadcast_to([P, B * E, CAP]),
                            iota_s[:].unsqueeze(1).broadcast_to([P, B * E, CAP]), ALU.is_equal).then_inc(onehot_ok, 1)
            dve.wait_ge(onehot_ok, 1)
            v.tensor_tensor(weighted.rearrange("p e b s -> p b e s"), onehot,
                            by_batch(3).unsqueeze(3).broadcast_to([P, B, E, CAP]), ALU.mult).then_inc(weighted_ok, 1)
            for i in range(4):
                c = 2 * i
                dve.wait_ge(xin_mm, c + 1)
                v.tensor_copy(xin[:, c % 4].rearrange("p e (b s) -> p b e s", b=B)[:, 2 * (c // 4):2 * (c // 4) + 2],
                              banks[c].rearrange("p (b e s) -> p b e s", b=2, e=E)).then_inc(xin_dve, 1)
            dve.wait_ge(xin_hi_ok, 1)
            v.tensor_tensor(xin_lo[:], xin[:, :, 0], xin_hi[:], ALU.subtract).then_inc(xin_staged, 1)
            for i in range(2):
                dve.wait_ge(back_mm, i + 1)
                v.tensor_reduce(gcol[:, 4 * i:4 * i + 4], ps[:, i].rearrange("p (e t) -> p e t", e=4), AX.X, ALU.add).then_inc(back_ok, 1)
                v.tensor_scalar(back[:, 4 * i:4 * i + 4].rearrange("p e t -> p (e t)"), ps[:, i], 0.0, None, ALU.is_gt).then_inc(back_ok, 1)
            def split_lo(e, i):
                dve.wait_ge(hi_ok, e * 8 + (i + 1))
                v.tensor_tensor(w_lo[:, i % SLOTS], att_w[:, i], w_hi[:, i % SLOTS], ALU.subtract).then_inc(lo_ok, 1)

            def transposed_lo(e, q):
                dve.wait_ge(ht_hi_ok, e * 4 + (q + 1))
                part = slice(q * 4, q * 4 + 4)
                v.tensor_tensor(ht_lo[:, part].rearrange("p c n -> p (c n)"), po[:, 1],
                                ht_hi[:, part].rearrange("p c n -> p (c n)"), ALU.subtract).then_inc(ht_lo_ok, 1)

            def expert(e, more):
                for q in range(NQ):
                    split_lo(e, NQ + q)
                    transposed_lo(e, q)
                if more:
                    for i in range(SLOTS - 1):
                        split_lo(e + 1, i)
                dve.wait_ge(tile_mm, e * 8 + 8)
                if isinstance(e, int) and e == 0:
                    dve.wait_ge(back_ok, 4)
                else:
                    dve.wait_ge(y_lo_ok, e)
                v.tensor_tensor(y_s[:], po[:, 0], gcol[:, bass.ds(e, 1)].broadcast_to([P, D]), ALU.mult).then_inc(y_ok, 1)
                if more:
                    split_lo(e + 1, SLOTS - 1)
                dve.wait_ge(y_hi_ok, e + 1)
                v.tensor_tensor(y_lo[:], y_s[:], y_hi[:], ALU.subtract).then_inc(y_lo_ok, 1)

            expert(0, True)
            with dve.Fori(1, E - 1) as e:
                expert(e, True)
            expert(E - 1, False)
            for b in range(B):
                dve.wait_ge(rounded_ok, b + 1)
                v.tensor_tensor(x_s[:, b], x_s[:, b], rounded[:, b], ALU.add).then_inc(res_ok, 1)

        @block.tensor
        def _(pe):
            mm = nc.tensor.matmul

            def k_project(t):
                pe.wait_ge(ctx_in, t * 16 + 16)
                if not isinstance(t, int):
                    pe.wait_ge(k_out, t)
                for g in range(KC):
                    for k in range(KC):
                        ins = mm(pk[:, g * P:(g + 1) * P], wk_s[:, k, g * P:(g + 1) * P], ctx_s[:, k], start=k == 0, stop=k == KC - 1)
                ins.then_inc(k_mm, 1)

            def v_project(t, k):
                if k == 0:
                    pe.wait_ge(ctx_lo_ok, t + 1)
                    if not isinstance(t, int):
                        pe.wait_ge(v_out, t)
                for c, w in ((ctx_hi, w_hi), (ctx_hi, w_lo), (ctx_lo, w_hi)):
                    ins = mm(pv[:], c[:, k], w[:, 1, k], start=k == 0 and c is ctx_hi and w is w_hi,
                             stop=k == KC - 1 and c is ctx_lo, skip_group_check=True)
                if k == KC - 1:
                    ins.then_inc(v_mm, 1)

            def turn_batch(i, b):
                pe.wait_ge(normed[i], b + 1)
                for k in range(KC):
                    ins = nc.tensor.transpose(turned(i, b)[:, k], norm[:, b, k * P:(k + 1) * P], ident[:])
                ins.then_inc(tr_mm[i], 1)

            def product(dst, pairs):
                for n, (l, r) in enumerate(pairs):
                    ins = mm(dst, l, r, start=n == 0, stop=n == len(pairs) - 1, skip_group_check=True)
                return ins

            def project_t(slot, dst, done):
                for g in range(KC):
                    cols_g = slice(g * P, (g + 1) * P)
                    product(dst[g], [(w[:, slot, k, cols_g], t[:, k]) for k in range(KC)
                                     for w, t in ((w_hi, tr_hi), (w_lo, tr_hi), (w_hi, tr_lo))]).then_inc(done, 1)

            def project(slot, b, dst, done):
                now = slice(b * T, (b + 1) * T)
                product(dst, [(t[:, k, now], w[:, slot, k]) for k in range(KC)
                              for w, t in ((w_hi, tr_hi), (w_lo, tr_hi), (w_hi, tr_lo))]).then_inc(done, 1)

            prime(pe, v_mm, s_mm)
            pe.wait_ge(consts, 11)
            pe.wait_ge(act_ok, 1)
            mm(pv[0:NJ, 0:1], tri[:], idx[:, 7:8], start=True, stop=True).then_inc(place_mm, 1)
            pe.wait_ge(pick_ok, 1)
            mm(pv[0:1, 0:NJ + 1], idx[:, 0:1], pick[:], start=True, stop=True)
            mm(pv[0:1, NJ + 1:2 * (NJ + 1)], idx[:, 2:3], pick[:], start=True, stop=True)
            mm(pv[0:1, 2 * (NJ + 1):2 * (NJ + 1) + 1], idx[:, 7:8], idx[:, 5:6], start=True, stop=True).then_inc(table_mm, 1)
            last = last_chunk(pe)
            def scores(t, is_last=False):
                pe.wait_ge(bias_in, t * 16 + 16)
                pe.wait_ge(q_staged, t + 1)
                pe.wait_ge(k_out, t + 1)
                pe.wait_ge(pt_dve, t * 3 + 1)
                pe.wait_ge(pt_act, t + 1)
                for c in range(STRIPS):
                    mm(ps[:, c].rearrange("p (g k) -> p g k", g=KC), ones3[:], bias3[:].unsqueeze(1).broadcast_to([P, KC, P]),
                       start=True, stop=False, skip_group_check=True)
                for g in range(KC):
                    if g == KC // 2:
                        v_project(t, KC - 1)
                        if is_last:
                            turn_batch(1, 0)
                    for c in range(STRIPS):
                        r = slice(c * DH, (c + 1) * DH)
                        ins = mm(ps[:, c, g * P:(g + 1) * P], q_now[r, g], kt_s[r, g], start=False, stop=True, skip_group_check=True)
                ins.then_inc(s_mm, 1)

            def turn_probs(t, c):
                pe.wait_ge(p_ok, t * 4 + (c + 1))
                for g in range(KC):
                    ins = nc.tensor.transpose(ps[:, c, g * P:(g + 1) * P], big_a[:, c * KC + g], ident[:])
                ins.then_inc(pt_mm, 1)

            def values(t, c):
                if c == 0:
                    pe.wait_ge(v_out, t + 1)
                    pe.wait_ge(summed, t + 1)
                if c < 3:
                    pe.wait_ge(pt_dve, t * 3 + (c + 2))
                else:
                    pe.wait_ge(pt_act, t + 2)
                for h in range(c * KC, (c + 1) * KC):
                    ins = mm(po[:, h // 8, (h % 8) * HV:(h % 8 + 1) * HV], big_b[:, h], v_s[:, 0, h], start=True, stop=True)
                if c == 3:
                    ins.then_inc(pv_mm, 1)

            def chunk(t):
                scores(t)
                k_project(t + 1)
                v_project(t + 1, 0)
                turn_probs(t, 0)
                v_project(t + 1, 1)
                turn_probs(t, 1)
                values(t, 0)
                turn_probs(t, 2)
                v_project(t + 1, 2)
                values(t, 1)
                turn_probs(t, 3)
                values(t, 2)
                values(t, 3)

            pe.wait_ge(in_wk, 16)
            for b in range(B):
                turn_batch(0, b)
            k_project(0)
            pe.wait_ge(tr_lo_ok[0], B)
            pe.wait_ge(att_lo_ok, 1)
            project_t(2, banks[0:4], q_mm)
            pe.wait_ge(att_lo_ok, 2)
            for k in range(KC - 1):
                v_project(0, k)
            pe.wait_ge(q_out, 4)
            with pe.Fori(0, last) as t:
                chunk(t)

            def cross_project(b):
                pe.wait_ge(tr_lo_ok[1], b + 1)
                pe.wait_ge(att_lo_ok, 4)
                if b >= 2:
                    pe.wait_ge(o_out, b - 1)
                project(2, b, banks[CROSS_BANKS[b]], o_mm)

            def values_project(b):
                pe.wait_ge(tr_lo_ok[2], b + 1)
                project(1, b, banks[V2_BANKS[b]], v2_mm)

            scores(last, is_last=True)
            pe.wait_ge(v_out, last + 1)
            turn_batch(1, 1)
            turn_batch(1, 2)
            cross_project(0)
            turn_probs(last, 0)
            turn_probs(last, 1)
            cross_project(1)
            pe.wait_ge(tr_lo_ok[1], B - 1)
            values(last, 0)
            turn_probs(last, 2)
            values(last, 1)
            turn_probs(last, 3)
            values(last, 2)
            values(last, 3)
            turn_batch(2, 0)
            cross_project(2)
            turn_batch(1, 3)
            pe.wait_ge(att_lo_ok, 5)
            values_project(0)
            turn_batch(2, 1)
            cross_project(3)
            turn_batch(2, 2)
            values_project(1)
            turn_batch(2, 3)
            values_project(2)
            pe.wait_ge(tr_lo_ok[2], B)
            project_t(3, banks[4:8], q2_mm)
            pe.wait_ge(v2_out, B - 1)
            pe.wait_ge(att_lo_ok, 6)
            project_t(0, banks[0:4], k2_mm)
            pe.wait_ge(q2_act, 1)
            values_project(3)

            def waits_scores2(u):
                pe.wait_ge(wide_ok, 4 * (u // 2 + 1))
                if u == 0:
                    pe.wait_ge(q2_out, KC)
                    pe.wait_ge(k2_out, KC)
                if u >= 2:
                    pe.wait_ge(s2_clamped, u - 1)

            def waits_values2(u):
                pe.wait_ge(e2_ok, u + 1)
                if u == 0:
                    pe.wait_ge(v2_out, B)
                if u >= 2:
                    pe.wait_ge(pv2_out, u - 1)

            def score2(u, n):
                b, g, c = u // 2, n // 2, 2 * (u % 2) + n % 2
                return mm(ps[:, c, g * P:(g + 1) * P], kt2[:, b, g], q_wide[:, b % 2, c, g], start=True, stop=True)

            def value2(u, n):
                b, c = u // 2, u % 2
                half = big_a if c == 0 else big_b
                return mm(po[:, c, n * HV:(n + 1) * HV], half[:, 8 + n], v_s[:, b, 8 * c + n], start=True, stop=True)

            def unit(u):
                waits_values2(u)
                more = u + 2 < 2 * B
                if more:
                    waits_scores2(u + 2)
                for n in range(8):
                    if more:
                        ins = score2(u + 2, n)
                        if n == 7:
                            ins.then_inc(s2_mm, 1)
                    ins = value2(u, n)
                ins.then_inc(pv2_mm, 1)

            def out_project(b):
                pe.wait_ge(tr_lo_ok[3], b + 1)
                pe.wait_ge(att_lo_ok, 7)
                if b:
                    pe.wait_ge(o2_out, b)
                project(3, b, pv[:], o2_mm)

            def turn_out(b):
                if b == 1:
                    pe.wait_ge(tr_lo_ok[3], 1)
                if b >= 2:
                    pe.wait_ge(tr_hi_ok[4], b - 1)
                turn_batch(3, b)

            def turn_gate(b):
                pe.wait_ge(tr_lo_ok[3], min(b + 2, B))
                if b == B - 1:
                    pe.wait_ge(tr_hi_ok[4], b)
                turn_batch(4, b)

            def gate_project(b, u):
                pe.wait_ge(tr_hi_ok[4], b + 1)
                pe.wait_ge(pv2_out, u)
                for k in range(KC):
                    ins = mm(logits[:, b * E:(b + 1) * E], tr_gate[:, b, k], gate_s[:, k], start=k == 0, stop=k == KC - 1)
                ins.then_inc(g_mm, 1)

            pe.wait_ge(in_gate, 16)
            for u in range(2):
                waits_scores2(u)
                for n in range(8):
                    ins = score2(u, n)
                ins.then_inc(s2_mm, 1)
            for u in range(2 * B):
                unit(u)
                if u == 2:
                    turn_out(0)
                if u == 3:
                    out_project(0)
                    turn_out(1)
                if u == 5:
                    turn_gate(0)
                    out_project(1)
                    turn_out(2)
                if u == 6:
                    out_project(2)
                    turn_gate(1)
            turn_out(3)
            gate_project(0, 2 * B)
            gate_project(1, 2 * B)
            out_project(3)
            turn_gate(2)
            gate_project(2, 2 * B)
            turn_gate(3)
            gate_project(3, 2 * B)
            pe.wait_ge(g_ok, 1)
            nc.tensor.transpose(pv[0:B * E, 0:T], gsm[:, 3], ident[:]).then_inc(pt_g, 1)
            pe.wait_ge(slot_ok, 1)
            nc.tensor.transpose(pk[:, 0:B * E], chosen[:, 2], ident[0:B * E, 0:B * E]).then_inc(slot_mm, 1)
            pe.wait_ge(onehot_ok, 1)
            pe.wait_ge(norm_lo_ok, B)
            for c in range(8):
                k, pair = c % 4, c // 4
                for b in (2 * pair, 2 * pair + 1):
                    for part in (norm_hi, norm_lo):
                        ins = mm(banks[c][:, (b % 2) * E * CAP:(b % 2 + 1) * E * CAP], part[:, b, k * P:(k + 1) * P],
                                 onehot[:, b].rearrange("p e s -> p (e s)"), start=part is norm_hi, stop=part is norm_lo,
                                 skip_group_check=True)
                ins.then_inc(xin_mm, 1)
            pe.wait_ge(weighted_ok, 1)
            pe.wait_ge(xin_dve, 4)
            pe.wait_ge(xin_act, 4)
            for e in range(E):
                ins = nc.tensor.transpose(ps[:, e // 4, (e % 4) * T:(e % 4 + 1) * T], weighted[:, e].rearrange("p b s -> p (b s)"), ident[:])
                if e % 4 == 3:
                    ins.then_inc(back_mm, 1)

            def passes(dst, left_hi, left_lo, slot, q, start):
                terms = [(l[:, c], r[:, slot, c - q]) for c in range(q, q + KC)
                         for l, r in ((left_hi, w_hi), (left_hi, w_lo), (left_lo, w_hi))]
                for i, (l, r) in enumerate(terms):
                    ins = mm(dst, l, r, start=start and i == 0, stop=i == len(terms) - 1, skip_group_check=True)
                return ins

            def hidden(e, q):
                if q == 0:
                    pe.wait_ge(xin_staged, e + 1)
                pe.wait_ge(lo_ok, SLOTS if isinstance(e, int) and e == 0 else e * 8 + (q + 1))
                if q >= 2 or not isinstance(e, int):
                    pe.wait_ge(gelu_ok, e * 4 + (q - 1))
                passes((pk, pv)[q % 2][:], xin_hi, xin_lo, q % SLOTS, 0, True).then_inc(tile_mm, 1)

            def turn(e, q):
                pe.wait_ge(gelu_ok, e * 4 + (q + 1))
                if q or not isinstance(e, int):
                    pe.wait_ge(ht_lo_ok, e * 4 + q)
                for c in range(KC):
                    ins = nc.tensor.transpose(po[:, 1, c * P:(c + 1) * P], h_s[:, q % 2, c * P:(c + 1) * P], ident[:])
                ins.then_inc(ht_mm, 1)

            def expert_out(e, q):
                pe.wait_ge(lo_ok, e * 8 + (NQ + q + 1))
                pe.wait_ge(ht_lo_ok, e * 4 + (q + 1))
                if q == 0 and not isinstance(e, int):
                    pe.wait_ge(y_ok, e)
                passes(po[:, 0], ht_hi, ht_lo, q % SLOTS, q * KC, q == 0).then_inc(tile_mm, 1)

            def scatter(e, at_end=False):
                pe.wait_ge(back_staged, e + 1)
                pe.wait_ge(y_lo_ok, e + 1)
                first = isinstance(e, int) and e == 0
                steps = [(b, y) for y in (y_hi, y_lo) for b in range(B)]
                if at_end:
                    steps = [(b, y) for b in range(B) for y in (y_hi, y_lo)]
                for b, y in steps:
                    r = slice(b * CAP, (b + 1) * CAP)
                    ins = mm(ps[:, b], back_now[r], y[r], start=first and y is y_hi, stop=False, skip_group_check=True)
                    if at_end and y is y_lo:
                        ins.then_inc(summed_up, 1)
                if not at_end:
                    ins.then_inc(sc_mm, 1)

            def expert(e, before):
                hidden(e, 0)
                hidden(e, 1)
                turn(e, 0)
                if before is not None:
                    scatter(before)
                hidden(e, 2)
                turn(e, 1)
                hidden(e, 3)
                turn(e, 2)
                expert_out(e, 0)
                turn(e, 3)
                for q in range(1, NQ):
                    expert_out(e, q)

            expert(0, None)
            expert(1, 0)
            with pe.Fori(2, E) as e:
                expert(e, e - 1)
            scatter(E - 1, at_end=True)


_INS = ["x", "ctx_t", "key_bias", "key_mask", "wq", "bq", "wk", "bk", "wv", "bv", "wo", "bo",
        "sq", "sbq", "sk", "sbk", "sv", "sbv", "so", "sbo", "gate", "w1", "w2"]


def kernel(**inputs):
    import numpy as np
    import concourse.bacc as bacc
    from concourse.bass_utils import run_bass_kernel_spmd

    a = {k: np.asarray(v) for k, v in inputs.items()}

    def columns(v):
        return v.reshape(KC, P).T

    kv_w, kv_b = a["L0_xattn_Wkv_w"], a["L0_xattn_Wkv_b"]
    laid = {
        "x": a["x"],
        "ctx_t": a["ctx_1024"].reshape(NJ, P, KC, P).transpose(0, 3, 2, 1),
        "key_bias": a["fside_BxS2_0"].reshape(NJ, P),
        "key_mask": a["mask_BxS2_bk0"].reshape(NJ, P),
        "wq": a["L0_xattn_Wq_w"].T, "bq": columns(a["L0_xattn_Wq_b"]),
        "wk": kv_w[:D].T, "bk": columns(kv_b[:D]),
        "wv": kv_w[D:].T, "bv": kv_b[D:],
        "wo": a["L0_xattn_out_w"].T, "bo": a["L0_xattn_out_b"],
        "sq": a["L0_attn_Wq"].T, "sbq": columns(a["L0_attn_bq"]),
        "sk": a["L0_attn_Wk"].T, "sbk": columns(a["L0_attn_bk"]),
        "sv": a["L0_attn_Wv"].T, "sbv": a["L0_attn_bv"],
        "so": a["L0_attn_Wo"].T, "sbo": a["L0_attn_bo"],
        "gate": a["L0_ffn_gate_w"], "w1": a["L0_ffn_w1"], "w2": a["L0_ffn_w2"],
    }
    nc = bacc.Bacc("TRN2", target_bir_lowering=False, num_devices=1, dynamic_dma_scratch_size=1024)
    arrays, args = {}, []
    for name in _INS:
        v = np.ascontiguousarray(laid[name])
        arrays[f"in_{name}"] = v
        args.append(nc.dram_tensor(f"in_{name}", v.shape, mybir.dt.from_np(v.dtype), kind="ExternalInput").ap())
    args.append(nc.dram_tensor("out", (B, T, D), F32, kind="ExternalOutput").ap())
    decoder_layer(nc, *args)
    r = run_bass_kernel_spmd(nc, [arrays], core_ids=[0])
    return r.results[0]["out"]
```
